# Optimizing a Trainium2 kernel written in Bass

```python
import numpy as np
import jax
import jax.numpy as jnp

def _softmax(x, axis=-1):
    return jax.nn.softmax(x, axis=axis)

def _gelu(x):
    return jax.nn.gelu(x, approximate=True)

def _silu(x):
    return jax.nn.silu(x)

def _sigmoid(x):
    return jax.nn.sigmoid(x)

def _layernorm(x, axis=-1, eps=1e-05):
    m = jnp.mean(x, axis=axis, keepdims=True)
    v = jnp.var(x, axis=axis, keepdims=True)
    return (x - m) / jnp.sqrt(v + eps)

def _scatter_add(tgt, idx, src, axis=0):
    return tgt.at[idx].add(src)

def _segment_sum(src, seg, n):
    return jax.ops.segment_sum(src, seg, n)
kernel_name = 'mk_adaln_d1_jaxref_r8_3aa023'

def setup_inputs(seed: int=0):
    np.random.seed(seed)
    _w = jnp.asarray

    def _L0_attn_setup():
        import jax, jax.numpy as jnp
        import numpy as np
        import math
        H = 256
        B = 4
        T = 256
        LAYER_ID = 0
        N_LAYERS = 24

        def _init_params(key):
            ratio_0_to_1 = LAYER_ID / (N_LAYERS - 1)
            ratio_1_to_0 = 1.0 - LAYER_ID / N_LAYERS
            d = jnp.arange(H, dtype=jnp.float32) / max(H - 1, 1)
            tmk = jnp.power(d, ratio_1_to_0).reshape(1, 1, H)
            tmv = jnp.clip(jnp.power(d, ratio_1_to_0) + 0.3 * ratio_0_to_1, 0.0, 1.0).reshape(1, 1, H)
            tmr = jnp.power(d, 0.5 * ratio_1_to_0).reshape(1, 1, H)
            frac = jnp.arange(H, dtype=jnp.float32) / max(H - 1, 1)
            time_decay = -5.0 + 8.0 * jnp.power(frac, 0.7 + 1.3 * ratio_0_to_1)
            zigzag = ((jnp.arange(H) + 1) % 3 - 1).astype(jnp.float32) * 0.5
            time_first = jnp.full((H,), math.log(0.3), dtype=jnp.float32) + zigzag
            ks = jax.random.split(key, 4)
            lim = math.sqrt(6.0 / (H + H))
            Wk = jax.random.uniform(ks[0], (H, H), jnp.float32, -lim, lim)
            Wv = jax.random.uniform(ks[1], (H, H), jnp.float32, -lim, lim)
            Wr = jax.random.uniform(ks[2], (H, H), jnp.float32, -lim, lim)
            Wo = jax.random.normal(ks[3], (H, H), jnp.float32) * (0.02 / math.sqrt(N_LAYERS))
            z = jnp.zeros((H,), jnp.float32)
            return dict(Wk=Wk, bk=z, Wv=Wv, bv=z, Wr=Wr, br=z, Wo=Wo, bo=z, tmk=tmk, tmv=tmv, tmr=tmr, time_decay=time_decay, time_first=time_first)

        def _wkv_scan(k, v, time_decay, time_first):
            decay = -jnp.exp(time_decay)
            bonus = time_first
            b, t, h = k.shape
            aa0 = jnp.zeros((b, h), jnp.float32)
            bb0 = jnp.zeros((b, h), jnp.float32)
            pp0 = jnp.full((b, h), -1e+30, jnp.float32)

            def step(carry, kv):
                aa, bb, pp = carry
                kt, vt = kv
                ww = bonus + kt
                p = jnp.maximum(pp, ww)
                e1 = jnp.exp(pp - p)
                e2 = jnp.exp(ww - p)
                out = (e1 * aa + e2 * vt) / (e1 * bb + e2)
                ww2 = pp + decay
                p2 = jnp.maximum(ww2, kt)
                e1 = jnp.exp(ww2 - p2)
                e2 = jnp.exp(kt - p2)
                return ((e1 * aa + e2 * vt, e1 * bb + e2, p2), out)
            kT = jnp.swapaxes(k, 0, 1)
            vT = jnp.swapaxes(v, 0, 1)
            _, outs = jax.lax.scan(step, (aa0, bb0, pp0), (kT, vT))
            return jnp.swapaxes(outs, 0, 1)
        key = jax.random.key(seed)
        kx, kp = jax.random.split(key)
        inp = {'x': jax.random.normal(kx, (B, T, H), jnp.float32)}
        inp.update(_init_params(kp))
        return inp
    _L0_attn_in = _L0_attn_setup()

    def _L0_ffn_setup():
        import jax, jax.numpy as jnp
        import numpy as np
        H = 256
        M = 64
        E = 8
        TOP_K = 2
        N_SHARED = 2
        MS = M * N_SHARED
        B, S = (2, 128)
        key = jax.random.key(seed)
        ks = jax.random.split(key, 9)
        sc = 0.02
        return {'hidden_states': jax.random.normal(ks[0], (B, S, H), dtype=jnp.float32), 'gate_w': jax.random.normal(ks[1], (E, H), dtype=jnp.float32) * sc, 'Wg': jax.random.normal(ks[2], (E, H, M), dtype=jnp.float32) * sc, 'Wu': jax.random.normal(ks[3], (E, H, M), dtype=jnp.float32) * sc, 'Wd': jax.random.normal(ks[4], (E, M, H), dtype=jnp.float32) * sc, 'sWg': jax.random.normal(ks[5], (H, MS), dtype=jnp.float32) * sc, 'sWu': jax.random.normal(ks[6], (H, MS), dtype=jnp.float32) * sc, 'sWd': jax.random.normal(ks[7], (MS, H), dtype=jnp.float32) * sc}
    _L0_ffn_in = _L0_ffn_setup()
    _L0_c = _w((lambda *s: np.random.randn(*s).astype(np.float32) * 0.05)(4, 256))
    _L0_wmod = _w((lambda *s: np.random.randn(*s).astype(np.float32) * 0.05)(256, 6 * 256) * 256 ** (-0.5))
    _d = {'L0_attn_x': _L0_attn_in['x'], 'L0_attn_Wk': _L0_attn_in['Wk'], 'L0_attn_bk': _L0_attn_in['bk'], 'L0_attn_Wv': _L0_attn_in['Wv'], 'L0_attn_bv': _L0_attn_in['bv'], 'L0_attn_Wr': _L0_attn_in['Wr'], 'L0_attn_br': _L0_attn_in['br'], 'L0_attn_Wo': _L0_attn_in['Wo'], 'L0_attn_bo': _L0_attn_in['bo'], 'L0_attn_tmk': _L0_attn_in['tmk'], 'L0_attn_tmv': _L0_attn_in['tmv'], 'L0_attn_tmr': _L0_attn_in['tmr'], 'L0_attn_time_decay': _L0_attn_in['time_decay'], 'L0_attn_time_first': _L0_attn_in['time_first'], 'L0_ffn_gate_w': _L0_ffn_in['gate_w'], 'L0_ffn_Wg': _L0_ffn_in['Wg'], 'L0_ffn_Wu': _L0_ffn_in['Wu'], 'L0_ffn_Wd': _L0_ffn_in['Wd'], 'L0_ffn_sWg': _L0_ffn_in['sWg'], 'L0_ffn_sWu': _L0_ffn_in['sWu'], 'L0_ffn_sWd': _L0_ffn_in['sWd'], 'L0_c': _L0_c, 'L0_wmod': _L0_wmod}
    _x0 = _d['L0_attn_x']
    _d['L0_attn_x'] = jax.random.normal(jax.random.fold_in(jax.random.key(seed), 1), (4, 1024, 256), dtype=_x0.dtype)
    del _x0
    return _d

def reference(L0_attn_x, L0_attn_Wk, L0_attn_bk, L0_attn_Wv, L0_attn_bv, L0_attn_Wr, L0_attn_br, L0_attn_Wo, L0_attn_bo, L0_attn_tmk, L0_attn_tmv, L0_attn_tmr, L0_attn_time_decay, L0_attn_time_first, L0_ffn_gate_w, L0_ffn_Wg, L0_ffn_Wu, L0_ffn_Wd, L0_ffn_sWg, L0_ffn_sWu, L0_ffn_sWd, L0_c, L0_wmod):

    def _L0_attn_ref(x, Wk, bk, Wv, bv, Wr, br, Wo, bo, tmk, tmv, tmr, time_decay, time_first):
        import jax, jax.numpy as jnp
        import numpy as np
        import math
        H = 256
        B = 4
        T = 256
        LAYER_ID = 0
        N_LAYERS = 24

        def _init_params(key):
            ratio_0_to_1 = LAYER_ID / (N_LAYERS - 1)
            ratio_1_to_0 = 1.0 - LAYER_ID / N_LAYERS
            d = jnp.arange(H, dtype=jnp.float32) / max(H - 1, 1)
            tmk = jnp.power(d, ratio_1_to_0).reshape(1, 1, H)
            tmv = jnp.clip(jnp.power(d, ratio_1_to_0) + 0.3 * ratio_0_to_1, 0.0, 1.0).reshape(1, 1, H)
            tmr = jnp.power(d, 0.5 * ratio_1_to_0).reshape(1, 1, H)
            frac = jnp.arange(H, dtype=jnp.float32) / max(H - 1, 1)
            time_decay = -5.0 + 8.0 * jnp.power(frac, 0.7 + 1.3 * ratio_0_to_1)
            zigzag = ((jnp.arange(H) + 1) % 3 - 1).astype(jnp.float32) * 0.5
            time_first = jnp.full((H,), math.log(0.3), dtype=jnp.float32) + zigzag
            ks = jax.random.split(key, 4)
            lim = math.sqrt(6.0 / (H + H))
            Wk = jax.random.uniform(ks[0], (H, H), jnp.float32, -lim, lim)
            Wv = jax.random.uniform(ks[1], (H, H), jnp.float32, -lim, lim)
            Wr = jax.random.uniform(ks[2], (H, H), jnp.float32, -lim, lim)
            Wo = jax.random.normal(ks[3], (H, H), jnp.float32) * (0.02 / math.sqrt(N_LAYERS))
            z = jnp.zeros((H,), jnp.float32)
            return dict(Wk=Wk, bk=z, Wv=Wv, bv=z, Wr=Wr, br=z, Wo=Wo, bo=z, tmk=tmk, tmv=tmv, tmr=tmr, time_decay=time_decay, time_first=time_first)

        def _wkv_scan(k, v, time_decay, time_first):
            decay = -jnp.exp(time_decay)
            bonus = time_first
            b, t, h = k.shape
            aa0 = jnp.zeros((b, h), jnp.float32)
            bb0 = jnp.zeros((b, h), jnp.float32)
            pp0 = jnp.full((b, h), -1e+30, jnp.float32)

            def step(carry, kv):
                aa, bb, pp = carry
                kt, vt = kv
                ww = bonus + kt
                p = jnp.maximum(pp, ww)
                e1 = jnp.exp(pp - p)
                e2 = jnp.exp(ww - p)
                out = (e1 * aa + e2 * vt) / (e1 * bb + e2)
                ww2 = pp + decay
                p2 = jnp.maximum(ww2, kt)
                e1 = jnp.exp(ww2 - p2)
                e2 = jnp.exp(kt - p2)
                return ((e1 * aa + e2 * vt, e1 * bb + e2, p2), out)
            kT = jnp.swapaxes(k, 0, 1)
            vT = jnp.swapaxes(v, 0, 1)
            _, outs = jax.lax.scan(step, (aa0, bb0, pp0), (kT, vT))
            return jnp.swapaxes(outs, 0, 1)
        x_prev = jnp.concatenate([jnp.zeros_like(x[:, :1, :]), x[:, :-1, :]], axis=1)
        xk = x_prev + (x - x_prev) * tmk
        xv = x_prev + (x - x_prev) * tmv
        xr = x_prev + (x - x_prev) * tmr
        k = jnp.einsum('bth,oh->bto', xk, Wk) + bk
        v = jnp.einsum('bth,oh->bto', xv, Wv) + bv
        r = jnp.einsum('bth,oh->bto', xr, Wr) + br
        wkv = _wkv_scan(k, v, time_decay, time_first)
        rwkv = jax.nn.sigmoid(r) * wkv
        out = jnp.einsum('bth,oh->bto', rwkv, Wo) + bo
        return out

    def _L0_ffn_ref(hidden_states, gate_w, Wg, Wu, Wd, sWg, sWu, sWd):
        import jax, jax.numpy as jnp
        import numpy as np
        H = 256
        M = 64
        E = 8
        TOP_K = 2
        N_SHARED = 2
        MS = M * N_SHARED
        B, S = (2, 128)
        b, s, h = hidden_states.shape
        x = hidden_states.reshape(-1, h)
        n = x.shape[0]
        logits = x @ gate_w.T
        topk_vals, topk_idx = jax.lax.top_k(logits, TOP_K)
        w = jax.nn.softmax(topk_vals, axis=-1)
        comb = jnp.zeros((n, E), x.dtype).at[jnp.arange(n)[:, None], topk_idx].add(w)
        g = jnp.einsum('nh,ehm->enm', x, Wg)
        u = jnp.einsum('nh,ehm->enm', x, Wu)
        eo = jnp.einsum('enm,emh->enh', jax.nn.silu(g) * u, Wd)
        y = jnp.einsum('ne,enh->nh', comb, eo)
        y = y + jax.nn.silu(x @ sWg) * (x @ sWu) @ sWd
        return y.reshape(b, s, h)
    x = L0_attn_x
    mod = (_silu(L0_c) @ L0_wmod).reshape(L0_c.shape[0], 6, 1, -1)
    sa, ca, ga, sb, cb, gb = (mod[:, 0], mod[:, 1], mod[:, 2], mod[:, 3], mod[:, 4], mod[:, 5])
    ga = (2 * (ga >= 0) - 1) * jnp.maximum(jnp.abs(ga), 0.25)
    gb = (2 * (gb >= 0) - 1) * jnp.maximum(jnp.abs(gb), 0.25)
    h = _layernorm(x, axis=-1) * (1 + ca) + sa
    x = x + ga * _L0_attn_ref(h, L0_attn_Wk, L0_attn_bk, L0_attn_Wv, L0_attn_bv, L0_attn_Wr, L0_attn_br, L0_attn_Wo, L0_attn_bo, L0_attn_tmk, L0_attn_tmv, L0_attn_tmr, L0_attn_time_decay, L0_attn_time_first)
    h = _layernorm(x, axis=-1) * (1 + cb) + sb
    x = x + gb * _L0_ffn_ref(h, L0_ffn_gate_w, L0_ffn_Wg, L0_ffn_Wu, L0_ffn_Wd, L0_ffn_sWg, L0_ffn_sWu, L0_ffn_sWd)
    return x

_drawn_inputs = setup_inputs


def setup_inputs(seed=0):
    import zlib

    import numpy as np

    out = dict(_drawn_inputs(seed))
    spreads = {'L0_attn_bk': (0.0, 2.0),
     'L0_attn_bv': (0.0, 2.0),
     'L0_attn_br': (0.0, 0.8),
     'L0_attn_bo': (0.0, 1.026)}
    factors = {'L0_attn_Wk': 8.0,
     'L0_attn_Wv': 8.0,
     'L0_attn_Wr': 8.0,
     'L0_attn_Wo': 8.0,
     'L0_attn_tmk': 8.0,
     'L0_attn_tmv': 8.0,
     'L0_attn_tmr': 8.0,
     'L0_attn_time_decay': 8.0,
     'L0_attn_time_first': 8.0,
     'L0_ffn_gate_w': 8.0,
     'L0_ffn_Wg': 8.0,
     'L0_ffn_Wu': 8.0,
     'L0_ffn_Wd': 8.0,
     'L0_ffn_sWg': 8.0,
     'L0_ffn_sWu': 8.0,
     'L0_ffn_sWd': 8.0}
    for name, (base, spread) in spreads.items():
        noise = np.random.default_rng([zlib.crc32(name.encode()), seed]).standard_normal(out[name].shape)
        drawn = base * np.exp(spread * noise) if base else spread * noise
        out[name] = jnp.asarray(drawn.astype(out[name].dtype))
    for name, factor in factors.items():
        out[name] = (out[name] * factor).astype(out[name].dtype)
    return out
```

```python
from collections import namedtuple
from contextlib import ExitStack

import concourse.bass as bass
from concourse import mybir

ALU = mybir.AluOpType
ACT = mybir.ActivationFunctionType
AX = mybir.AxisListType
F32 = mybir.dt.float32
F32R = mybir.dt.float32r

P = 128
B, T, H = 4, 1024, 256
KH = H // P
CH = 512
TT = CH // P
NC = B * T // CH
E, M = 8, 64
NB = E * M // P + 1
NP = NB - 1
EPS = 1e-5
START = -1e30
K, V, R, O = range(4)

EXP_SET = "natural_log_exp_and_others"
SILU_SET = "silu_and_others"

Chunk = namedtuple("Chunk", "n batch half")


def chunk(n):
    return Chunk(n, n // 2, n % 2)


def chunk_in_loop(i, offset):
    return Chunk(2 * i + offset, i + offset // 2, offset % 2)


def adaln_rwkv_moe(nc, x, Wk, bk, Wv, bv, Wr, br, Wo, bo, tmk, tmv, tmr, time_decay, time_first,
                   gate_w, Wg, Wu, Wd, sWg, sWu, sWd, cond, wmod, out):
    x_chunks = x.rearrange("b (g t p) h -> (b g) p t h", t=TT, p=P)
    out_chunks = out.rearrange("b (g t p) h -> (b g) p t h", t=TT, p=P)

    with ExitStack() as ctx:
        def sb(name, shape, dt=F32):
            return ctx.enter_context(nc.sbuf_tensor(name, shape, dt))

        def sem(name):
            return ctx.enter_context(nc.semaphore(name))

        ident = sb("ident", [P, P])
        ones_r = sb("ones_r", [P, P], F32R)
        sel = sb("sel", [2 * E, NP, P], F32R)
        prio = sb("prio", [P, TT, E])
        small = sb("small", [P, 3, TT])
        rows = sb("rows", [24, P])
        cols = sb("cols", [P, 24])
        condT = sb("condT", [P, 2 * B])
        decay = sb("decay", [P, KH])
        modc = sb("modc", [P, 4, KH, B])
        gb = sb("gb", [P, B, H])
        bo_b = sb("bo_b", [P, H])
        pace = sb("pace", [P, 1])
        mod1 = sb("mod1", [P, 2, KH])
        mod2 = sb("mod2", [P, 2, KH])
        bias_r = sb("bias_r", [P, B, H], F32R)
        WT = sb("WT", [P, 4, KH, H])
        WoG = sb("WoG", [P, B, KH, H])
        gw = sb("gw", [E, H])
        gwT = sb("gwT", [P, KH, E])
        w_up_h = sb("w_up_h", [P, KH, 2, NB * P], F32R)
        w_up_l = sb("w_up_l", [P, KH, 2, NB * P], F32R)
        WdG = sb("WdG", [P, B, NB, H])

        x_in = [sb(f"x_in{h}", [P, TT, H]) for h in range(2)]
        hT = [sb(f"hT{h}", [P, KH, CH + 1]) for h in range(2)]
        mixed = sb("mixed", [P, 3, KH, CH])
        kvr = sb("kvr", [P, 3, KH, CH])
        state = sb("state", [P, 3, KH, CH + 1])
        arg = sb("arg", [P, 4, KH, CH])
        ev = sb("ev", [P, KH, CH])
        tmp = sb("tmp", [P, KH, CH])
        h2_h = sb("h2_h", [P, KH, CH], F32R)
        h2_l = sb("h2_l", [P, KH, CH], F32R)
        rt = sb("rt", [P, 8, TT, E])
        r1 = sb("r1", [P, 8, TT])
        comb = sb("comb", [P, TT, 2 * E], F32R)
        combT = sb("combT", [2 * E, CH], F32R)
        pool_x = sb("pool_x", [P, 3 * TT * H])
        pool_n = sb("pool_n", [P, 2 * KH * CH])
        pool_g = sb("pool_g", [P, NB * CH])
        pool_a = sb("pool_a", [P, NB * CH])
        wmod_sb = pool_x[:, :].rearrange("p (k q) -> p k q", k=KH)
        x1 = [pool_x[:, h * TT * H:(h + 1) * TT * H].rearrange("p (t h) -> p t h", t=TT) for h in range(2)]
        h2 = pool_x[:, 2 * TT * H:].rearrange("p (k n) -> p k n", k=KH)
        w_nat = pool_n[:, :].rearrange("p (w a h) -> p w a h", w=4, a=KH)
        num = pool_n[:, 0:KH * CH].rearrange("p (k n) -> p k n", k=KH)
        den = pool_n[:, KH * CH:].rearrange("p (k n) -> p k n", k=KH)
        w_up = pool_g[:, :].rearrange("p (k g n) -> p k g n", k=KH, g=2)
        sg = pool_g[:, :].rearrange("p (e n) -> p e n", e=NB)
        w_dn = pool_a[:, 0:NB * H].rearrange("p (e h) -> p e h", e=NB)
        ga = pool_a[:, NB * H:NB * H + B * H].rearrange("p (b h) -> p b h", b=B)
        act = pool_a[:, :].rearrange("p (e n) -> p e n", e=NB)
        sel_f = tmp[0:2 * E, 0, :].rearrange("p (i n) -> p i n", i=NP)
        diff = tmp
        rec = arg[:, 0, :, :]
        sgm = kvr[:, R, :, :]
        rw = num

        mm = [ctx.enter_context(nc.psum_tensor(f"mm{i}", [P, CH], F32)) for i in range(4)]
        yo = [ctx.enter_context(nc.psum_tensor(f"yo{i}", [P, CH], F32)) for i in range(2)]
        tp = ctx.enter_context(nc.psum_tensor("tp", [P, CH], F32))
        cb = ctx.enter_context(nc.psum_tensor("cb", [P, CH], F32))

        class Norm:

            def __init__(self, name):
                self.stats = sb(f"{name}_stats", [P, TT, 6])
                self.mv = sb(f"{name}_mv", [P, TT, 2])
                self.ve = sb(f"{name}_ve", [P, TT])
                self.rstd = sb(f"{name}_rstd", [P, TT])
                self.mr = sb(f"{name}_mr", [P, TT])
                self.shift = sb(f"{name}_shift", [P, TT])
                self.xn = sb(f"{name}_xn", [P, TT, H])
                self.bn_done = sem(f"{name}_bn_done")
                self.mv_done = sem(f"{name}_mv_done")
                self.pool_step = sem(f"{name}_pool_step")
                self.rstd_done = sem(f"{name}_rstd_done")
                self.xn_done = sem(f"{name}_xn_done")
                self.turned = sem(f"{name}_turned")
                self.h_done = sem(f"{name}_h_done")

        norm1, norm2 = Norm("n1"), Norm("n2")
        gabo = ga
        gmag = norm2.xn[:, :, :].rearrange("p (b g) h -> p b g h", b=2)

        rows_in, cond_in, sq_in, up_in, dn_in, bo_in, gw_in = (
            sem(n) for n in ("rows_in", "cond_in", "sq_in", "up_in", "dn_in", "bo_in", "gw_in"))
        consts_done, ident_done, sel_done = sem("consts_done"), sem("ident_done"), sem("sel_done")
        init_done = sem("init_done")
        cols_turned, cols_done, cond_done, decay_done = (
            sem(n) for n in ("cols_turned", "cols_done", "cond_done", "decay_done"))
        modc_mm, modc_done, gates_mm, gates_step, gates_done = (
            sem(n) for n in ("modc_mm", "modc_done", "gates_mm", "gates_step", "gates_done"))
        bias_step, bias_done = sem("bias_step"), sem("bias_done")
        w_turned, wt_done, wog_done, gwt_done = (
            sem(n) for n in ("w_turned", "wt_done", "wog_done", "gwt_done"))
        up_hi_done, up_lo_done, wdg_done = sem("up_hi_done"), sem("up_lo_done"), sem("wdg_done")
        x_loaded = [sem(f"x_loaded{h}") for h in range(2)]
        stored = [sem(f"stored{h}") for h in range(2)]
        diff_done = sem("diff_done")
        mixed_done = sem("mixed_done")
        kvr_mm = sem("kvr_mm")
        kvr_done = sem("kvr_done")
        seed_done = sem("seed_done")
        pp_done = sem("pp_done")
        arg_done = sem("arg_done")
        relu_done = sem("relu_done")
        exp_done = sem("exp_done")
        ev_done = sem("ev_done")
        aabb_done = sem("aabb_done")
        part_done = sem("part_done")
        num_done = sem("num_done")
        den_done = sem("den_done")
        ln_done = sem("ln_done")
        rec_done = sem("rec_done")
        newton_done = sem("newton_done")
        sgm_done = sem("sgm_done")
        rw_done = sem("rw_done")
        wo_mm = sem("wo_mm")
        x1_done = sem("x1_done")
        h2lo_done = sem("h2lo_done")
        logits_mm = sem("logits_mm")
        route_step = sem("route_step")
        gap_done = sem("gap_done")
        gap_exp = sem("gap_exp")
        comb_done = sem("comb_done")
        comb_turned = sem("comb_turned")
        combT_done = sem("combT_done")
        comb_mm = sem("comb_mm")
        up_mm = sem("up_mm")
        silu_done = sem("silu_done")
        prod_done = sem("prod_done")
        act_done = sem("act_done")
        down_mm = sem("down_mm")
        x2_done = sem("x2_done")

        col = {n: cols[:, 2 * B + KH * i:2 * B + KH * (i + 1)]
               for i, n in enumerate(("tmk", "tmv", "tmr", "bk", "bv", "br", "td", "tf"))}
        mix_cols = (col["tmk"], col["tmv"], col["tmr"])
        bias_cols = (col["bk"], col["bv"], col["br"])
        mod1_done, mod2_done = sem("mod1_done"), sem("mod2_done")
        ROUTE_STEPS = 18

        block = ctx.enter_context(nc.Block())

        def wait(eng, s, value):
            if not (isinstance(value, int) and value <= 0):
                eng.wait_ge(s, value)

        @block.sync
        def _(sp):
            def load(c, first=False):
                if not first:
                    wait(sp, x1_done, 2 * (c.n - 1))
                sp.dma_start(x_in[c.half][:, :, :], x_chunks[c.n]).then_inc(x_loaded[c.half], 16)

            def store(c):
                wait(sp, x2_done, 2 * (c.n + 1))
                sp.dma_start(out_chunks[c.n], x1[c.half][:, :, :]).then_inc(stored[c.half], 16)

            load(chunk(0), first=True)
            for h in range(2):
                sp.sem_inc(stored[h], 16)
            for kc in range(KH):
                sp.dma_start(wmod_sb[:, kc, :], wmod[kc * P:(kc + 1) * P, :]).then_inc(cond_in, 16)
            load(chunk(1), first=True)
            sp.dma_start(bo_b[:, :], bo.rearrange("(a h) -> a h", a=1).to_broadcast([P, H])
                         ).then_inc(bo_in, 16)
            for kc in range(KH):
                sp.dma_start(w_up[:, kc, 0, 0:NP * P].rearrange("p (e m) -> p e m", m=M),
                             Wg[:, kc * P:(kc + 1) * P, :].rearrange("e p m -> p e m")).then_inc(up_in, 16)
                sp.dma_start(w_up[:, kc, 0, NP * P:], sWg[kc * P:(kc + 1) * P, :]).then_inc(up_in, 16)
            sp.dma_start(w_dn[:, 0:NP, :], Wd.rearrange("(i e) m h -> (e m) i h", e=2)).then_inc(dn_in, 16)
            sp.dma_start(w_dn[:, NP, :], sWd).then_inc(dn_in, 16)
            load(chunk(2))
            with sp.Fori(0, 2) as i:
                for offset in (0, 1):
                    load(chunk_in_loop(i, offset + 3))
                    store(chunk_in_loop(i, offset))
            load(chunk(NC - 1))
            for n in range(4, NC):
                store(chunk(n))
            for h in range(2):
                sp.wait_ge(stored[h], 16 * (NC // 2 + 1))

        @block.gpsimd
        def _(pool):
            nc.gpsimd.memset(ident[:, :], 0.0).then_inc(consts_done, 1)
            nc.gpsimd.memset(sel_f[:, :, :], 0.0).then_inc(consts_done, 1)
            nc.gpsimd.memset(small[:, 0, :], EPS).then_inc(consts_done, 1)
            nc.gpsimd.memset(small[:, 1, :], -0.5).then_inc(consts_done, 1)
            nc.gpsimd.memset(small[:, 2, :], 0.0).then_inc(consts_done, 1)
            pool.wait_ge(consts_done, 5)
            nc.gpsimd.affine_select(out=ident[:, :], in_=ident[:, :], compare_op=ALU.not_equal, fill=1.0,
                                    base=0, pattern=[[-1, P]], channel_multiplier=1).then_inc(ident_done, 1)
            for part in range(2):
                pool.wait_ge(sel_done, part) if part else None
                nc.gpsimd.affine_select(
                    out=sel_f[:, :, :].rearrange("p i (e m) -> p i e m", m=M),
                    in_=sel_f[:, :, :].rearrange("p i (e m) -> p i e m", m=M),
                    compare_op=ALU.not_equal, fill=1.0, base=-E * part,
                    pattern=[[-2, NP], [-1, 2], [0, M]], channel_multiplier=1).then_inc(sel_done, 1)

            def rstd(norm, c):
                wait(pool, norm.mv_done, TT * (c.n + 1))
                wait(pool, norm.xn_done, TT * c.n)
                nc.gpsimd.tensor_tensor(norm.ve[:, :], norm.mv[:, :, 1], small[:, 0, :], ALU.add
                                        ).then_inc(norm.pool_step, 1)
                pool.wait_ge(norm.pool_step, 3 * c.n + 1)
                nc.gpsimd.tensor_tensor(norm.rstd[:, :], norm.ve[:, :], small[:, 1, :], ALU.pow
                                        ).then_inc(norm.pool_step, 1)
                pool.wait_ge(norm.pool_step, 3 * c.n + 2)
                nc.gpsimd.tensor_tensor(norm.mr[:, :], norm.mv[:, :, 0], norm.rstd[:, :], ALU.mult
                                        ).then_inc(norm.pool_step, 1)
                pool.wait_ge(norm.pool_step, 3 * c.n + 3)
                nc.gpsimd.tensor_tensor(norm.shift[:, :], small[:, 2, :], norm.mr[:, :], ALU.subtract
                                        ).then_inc(norm.rstd_done, 1)

            rstd(norm1, chunk(0))
            pool.wait_ge(up_hi_done, 4)
            for kc in range(KH):
                for gu in range(2):
                    nc.gpsimd.tensor_tensor(w_up_l[:, kc, gu, :], w_up[:, kc, gu, :],
                                            w_up_h[:, kc, gu, :].bitcast(F32), ALU.subtract
                                            ).then_inc(up_lo_done, 1)
            rstd(norm1, chunk(1))
            pool.wait_ge(dn_in, 32)
            pool.wait_ge(gates_step, 8 * B)
            for b in range(B):
                for e in range(NB):
                    nc.gpsimd.tensor_tensor(WdG[:, b, e, :], w_dn[:, e, :], gb[:, b, :], ALU.mult
                                            ).then_inc(wdg_done, 1)
            rstd(norm2, chunk(0))
            with pool.Fori(0, 3) as i:
                for offset in (1, 2):
                    rstd(norm1, chunk_in_loop(i, offset + 1))
                    rstd(norm2, chunk_in_loop(i, offset))
            rstd(norm2, chunk(NC - 1))

        @block.scalar
        def _(ac):
            def normalise(norm, src, c, pick_mod=True):
                wait(ac, norm.rstd_done, c.n + 1)
                wait(ac, norm.turned, KH * c.n)
                for t in range(TT):
                    nc.scalar.activation(norm.xn[:, t, :], src[:, t, :], ACT.Identity,
                                         bias=norm.shift[:, t:t + 1], scale=norm.rstd[:, t:t + 1]
                                         ).then_inc(norm.xn_done, 1)
                if pick_mod:
                    pick(norm, c)

            def pick(norm, c):
                if c.half == 0:
                    mod, first, done = (mod1, 0, mod1_done) if norm is norm1 else (mod2, 2, mod2_done)
                    nc.scalar.activation(mod[:, :, :], modc[:, first:first + 2, :, bass.ds(c.batch, 1)]
                                         .rearrange("p q k b -> p q (k b)"), ACT.Identity).then_inc(done, 1)

            def affine1(c, kc):
                ac.wait_ge(norm1.turned, KH * c.n + kc + 1)
                wait(ac, mixed_done, 3 * KH * c.n)
                ac.wait_ge(mod1_done, c.batch + 1)
                scale, shift = mod1[:, 1, kc:kc + 1], mod1[:, 0, kc:kc + 1]
                last = nc.scalar.activation(hT[c.half][:, kc, 1:CH + 1], tp[:, :], ACT.Identity,
                                            bias=shift, scale=scale)
                if c.half == 0:
                    last = nc.scalar.activation(hT[1][:, kc, 0:1], tp[:, CH - 1:CH], ACT.Identity,
                                                bias=shift, scale=scale)
                last.then_inc(norm1.h_done, 1)

            def affine2(c):
                ac.wait_ge(mod2_done, c.batch + 1)
                for kc, src in ((0, tp), (1, cb)):
                    ac.wait_ge(norm2.turned, KH * c.n + kc + 1)
                    scale, shift = mod2[:, 1, kc:kc + 1], mod2[:, 0, kc:kc + 1]
                    nc.scalar.activation(h2_h[:, kc, :], src[:, :], ACT.Identity, bias=shift, scale=scale)
                    nc.scalar.activation(h2[:, kc, :], src[:, :], ACT.Identity, bias=shift, scale=scale
                                         ).then_inc(norm2.h_done, 1)

            def add_bias(c, j):
                w, kc = divmod(j, KH)
                ac.wait_ge(kvr_mm, 3 * KH * c.n + j + 1)
                nc.scalar.activation(kvr[:, w, kc, :], mm[j % 4][:, :], ACT.Identity,
                                     bias=bias_cols[w][:, kc:kc + 1]).then_inc(kvr_done, 1)

            def exponentials(c, h):
                for j in range(2):
                    ac.wait_ge(arg_done, 3 * (KH * c.n + h) + j + 1)
                    nc.scalar.activation(arg[:, j, h, :], arg[:, j, h, :], ACT.Exp).then_inc(exp_done, 1)
                ac.wait_ge(arg_done, 3 * (KH * c.n + h) + 3)
                nc.scalar.activation(arg[:, 2, h, :], tmp[:, h, :], ACT.Relu).then_inc(relu_done, 1)
                nc.scalar.activation(arg[:, 3, h, :], tmp[:, h, :], ACT.Relu, scale=-1.0
                                     ).then_inc(relu_done, 1)
                for j in range(2):
                    ac.wait_ge(relu_done, 2 * (KH * c.n + h) + j + 1)
                    nc.scalar.activation(arg[:, 2 + j, h, :], arg[:, 2 + j, h, :], ACT.Exp, scale=-1.0
                                         ).then_inc(exp_done, 1)

            def reciprocal_seed(c):
                for h in range(KH):
                    ac.wait_ge(den_done, KH * c.n + h + 1)
                    nc.scalar.activation(rec[:, h, :], den[:, h, :], ACT.Ln).then_inc(ln_done, 1)
                for h in range(KH):
                    ac.wait_ge(ln_done, KH * c.n + h + 1)
                    nc.scalar.activation(rec[:, h, :], rec[:, h, :], ACT.Exp, scale=-1.0
                                         ).then_inc(rec_done, 1)

            def tanh_r(c):
                ac.wait_ge(kvr_done, 3 * KH * (c.n + 1))
                for h in range(KH):
                    nc.scalar.activation(sgm[:, h, :], kvr[:, R, h, :], ACT.Tanh, scale=0.5
                                         ).then_inc(sgm_done, 1)

            def silu(c, e):
                ac.wait_ge(up_mm, 2 * (NB * c.n + e) + 1)
                nc.scalar.activation(sg[:, e, :], mm[(6 + 2 * e) % 4][:, :], ACT.Silu).then_inc(silu_done, 1)

            def project_and_scan(c, cur=None):
                add_bias(c, 0)
                add_bias(c, 1)
                if cur:
                    normalise(norm2, x1[cur.half], cur)
                add_bias(c, 2)
                exponentials(c, 0)
                add_bias(c, 3)
                add_bias(c, 4)
                exponentials(c, 1)
                add_bias(c, 5)
                if cur:
                    affine2(cur)
                    router(cur)
                reciprocal_seed(c)

            def router(c):
                ac.wait_ge(gap_done, c.n + 1)
                nc.scalar.activation(r1[:, 3, :], r1[:, 2, :], ACT.Exp).then_inc(gap_exp, 1)
                ac.wait_ge(comb_turned, c.n + 1)
                nc.scalar.activation(combT[:, :], tp[0:2 * E, :], ACT.Identity).then_inc(combT_done, 1)

            def step(prev, cur, nxt):
                nc.scalar.preload_act_table_set(SILU_SET)
                tanh_r(cur)
                if prev:
                    silu(prev, 0)
                if nxt:
                    normalise(norm1, x_in[nxt.half], nxt)
                if prev:
                    silu(prev, 1)
                    silu(prev, 2)
                if nxt:
                    affine1(nxt, 0)
                if prev:
                    silu(prev, 3)
                if nxt:
                    affine1(nxt, 1)
                if prev:
                    silu(prev, 4)
                nc.scalar.preload_act_table_set(EXP_SET)
                if nxt:
                    project_and_scan(nxt, cur)
                else:
                    normalise(norm2, x1[cur.half], cur)
                    affine2(cur)
                    router(cur)

            for r0, src in ((0, cond), (8, tmk), (10, tmv), (12, tmr), (14, bk), (16, bv), (18, br),
                            (20, time_decay), (22, time_first)):
                n = src.shape[0]
                ac.dma_start(rows[r0:r0 + n, :], src).then_inc(rows_in, 16)
            for w, src in enumerate((Wk, Wv, Wr, Wo)):
                ac.dma_start(w_nat[:, w, :, :], src.rearrange("(a p) h -> p a h", p=P)).then_inc(sq_in, 16)
            ac.dma_start(gw[:, :], gate_w).then_inc(gw_in, 16)
            for kc in range(KH):
                ac.dma_start(w_up[:, kc, 1, 0:NP * P].rearrange("p (e m) -> p e m", m=M),
                             Wu[:, kc * P:(kc + 1) * P, :].rearrange("e p m -> p e m")).then_inc(up_in, 16)
                ac.dma_start(w_up[:, kc, 1, NP * P:], sWu[kc * P:(kc + 1) * P, :]).then_inc(up_in, 16)
            nc.scalar.preload_act_table_set(SILU_SET)
            ac.wait_ge(cols_done, 1)
            nc.scalar.activation(condT[:, :], cols[:, 0:2 * B], ACT.Silu).then_inc(cond_done, 1)
            nc.scalar.preload_act_table_set(EXP_SET)
            nc.scalar.activation(decay[:, :], col["td"], ACT.Exp).then_inc(decay_done, 1)
            normalise(norm1, x_in[0], chunk(0), pick_mod=False)
            ac.wait_ge(modc_done, 4)
            pick(norm1, chunk(0))
            for kc in range(KH):
                affine1(chunk(0), kc)
            for w in range(4):
                ac.wait_ge(w_turned, w + 1)
                nc.scalar.activation(WT[:, w, :, :], mm[w][:, :].rearrange("p (k h) -> p k h", k=KH),
                                     ACT.Identity, scale=-0.5 if w == O else 1.0).then_inc(wt_done, 1)
            ac.wait_ge(w_turned, 5)
            nc.scalar.activation(gwT[:, :, :], cb[:, 0:KH * E].rearrange("p (k e) -> p k e", k=KH),
                                 ACT.Identity).then_inc(gwt_done, 1)
            project_and_scan(chunk(0))
            ac.wait_ge(up_in, 8 * 16)
            for kc in range(KH):
                for gu in range(2):
                    nc.scalar.activation(w_up_h[:, kc, gu, :], w_up[:, kc, gu, :], ACT.Identity
                                         ).then_inc(up_hi_done, 1)
            step(None, chunk(0), chunk(1))
            with ac.Fori(0, 3) as i:
                for offset in (1, 2):
                    step(*(chunk_in_loop(i, offset + d) for d in (-1, 0, 1)))
            step(chunk(NC - 2), chunk(NC - 1), None)
            nc.scalar.preload_act_table_set(SILU_SET)
            for e in range(NB):
                silu(chunk(NC - 1), e)

        @block.tensor
        def _(pe):
            def turn(norm, c, kc, dst):
                for t in range(TT):
                    last = nc.tensor.transpose(dst[:, t * P:(t + 1) * P], norm.xn[:, t, kc * P:(kc + 1) * P],
                                               ident[:, :])
                last.then_inc(norm.turned, 1)

            def turn1(c, kc):
                if kc == 0:
                    pe.wait_ge(norm1.xn_done, TT * (c.n + 1))
                    wait(pe, combT_done, c.n - 1)
                else:
                    pe.wait_ge(norm1.h_done, KH * c.n + 1)
                turn(norm1, c, kc, tp)

            def turn2(c):
                pe.wait_ge(norm2.xn_done, TT * (c.n + 1))
                turn(norm2, c, 0, tp)
                turn(norm2, c, 1, cb)

            def project(c, first=False):
                for j in range(3 * KH):
                    w, oc = divmod(j, KH)
                    if oc == 0:
                        pe.wait_ge(mixed_done, 3 * KH * c.n + KH * (w + 1))
                    if j >= 4:
                        pe.wait_ge(kvr_done, 3 * KH * c.n + j - 3)
                    elif not first:
                        if j % 2 == 0:
                            pe.wait_ge(silu_done, NB * (c.n - 2) + 4 + j // 2)
                        else:
                            pe.wait_ge(prod_done, NB * (c.n - 2) + 4 + j // 2)
                    for kc in range(KH):
                        last = nc.tensor.matmul(mm[j % 4][:, :], WT[:, w, kc, oc * P:(oc + 1) * P],
                                                mixed[:, w, kc, :], start=(kc == 0), stop=(kc == KH - 1))
                    last.then_inc(kvr_mm, 1)

            def output(c):
                pe.wait_ge(rw_done, KH * (c.n + 1))
                for t in range(TT):
                    dst = yo[t // 2][:, (t % 2) * H:(t % 2 + 1) * H]
                    nc.tensor.matmul(dst, ones_r[:, :], bias_r[:, c.batch, :], start=True, stop=False)
                    for kc in range(KH):
                        last = nc.tensor.matmul(dst, rw[:, kc, t * P:(t + 1) * P], WoG[:, c.batch, kc, :],
                                                start=False, stop=(kc == KH - 1))
                    if t % 2:
                        last.then_inc(wo_mm, 1)

            def logits(c):
                pe.wait_ge(norm2.h_done, KH * (c.n + 1))
                for t in range(TT):
                    for kc in range(KH):
                        last = nc.tensor.matmul(tp[:, t * E:(t + 1) * E], h2[:, kc, t * P:(t + 1) * P],
                                                gwT[:, kc, :], start=(kc == 0), stop=(kc == KH - 1))
                last.then_inc(logits_mm, 1)

            def turn_comb(c):
                pe.wait_ge(comb_done, c.n + 1)
                for t in range(TT):
                    last = nc.tensor.transpose(tp[0:2 * E, t * P:(t + 1) * P], comb[:, t, :].bitcast(F32),
                                               ident[:, :])
                last.then_inc(comb_turned, 1)

            def up(c, e, after_up=False):
                if e == 0:
                    pe.wait_ge(combT_done, c.n + 1)
                    pe.wait_ge(h2lo_done, KH * (c.n + 1))
                if e < NP:
                    if e:
                        pe.wait_ge(act_done, NP * c.n + e)
                    nc.tensor.matmul(cb[:, :], sel[:, e, :], combT[:, :], start=True, stop=True
                                     ).then_inc(comb_mm, 1)
                for gu in range(2):
                    i = 2 * e + gu
                    if i >= 4 or after_up:
                        wait(pe, prod_done if gu else silu_done, NB * c.n + e - 1 if i >= 4 else NB * c.n)
                    else:
                        pe.wait_ge(kvr_done, 3 * KH * (c.n + 1) + 3 + i)
                    n = 0
                    for w, rhs in ((w_up_h, h2_h), (w_up_h, h2_l), (w_up_l, h2_h)):
                        for kc in range(KH):
                            last = nc.tensor.matmul(mm[(6 + i) % 4][:, :], w[:, kc, gu, e * P:(e + 1) * P],
                                                    rhs[:, kc, :], start=(n == 0), stop=(n == 3 * KH - 1))
                            n += 1
                    last.then_inc(up_mm, 1)

            def down(c, tiles, last_chunk=False):
                if tiles[0] == 0:
                    pe.wait_ge(act_done, NP * (c.n + 1))
                    pe.wait_ge(prod_done, NB * (c.n + 1))
                    if last_chunk:
                        pe.wait_ge(x2_done, 2 * c.n)
                    else:
                        pe.wait_ge(x1_done, 2 * (c.n + 2))
                for t in tiles:
                    for e in range(NB):
                        last = nc.tensor.matmul(yo[t // 2][:, (t % 2) * H:(t % 2 + 1) * H],
                                                act[:, e, t * P:(t + 1) * P], WdG[:, c.batch, e, :],
                                                start=(e == 0), stop=(e == NB - 1))
                last.then_inc(down_mm, 1)

            def step(prev, cur, nxt):
                if prev:
                    for e in range(NB):
                        up(prev, e)
                        if nxt and e in (1, 3):
                            turn1(nxt, e // 2)
                elif nxt:
                    turn1(nxt, 0)
                    turn1(nxt, 1)
                output(cur)
                if nxt:
                    project(nxt)
                turn2(cur)
                logits(cur)
                if prev:
                    down(prev, (0, 1))
                turn_comb(cur)
                if prev:
                    down(prev, (2, 3))

            pe.wait_ge(ident_done, 1)
            pe.wait_ge(rows_in, 9 * 16)
            nc.tensor.transpose(mm[0][:, 0:24], rows[:, :], ident[0:24, 0:24]).then_inc(cols_turned, 1)
            pe.wait_ge(cond_done, 1)
            pe.wait_ge(cond_in, 2 * 16)
            for n, q in enumerate((0, 1, 3, 4)):
                for oc in range(KH):
                    for kc in range(KH):
                        at = (n * KH + oc) * B
                        last = nc.tensor.matmul(
                            mm[1][:, at:at + B], wmod_sb[:, kc, q * H + oc * P:q * H + (oc + 1) * P],
                            condT[:, :].rearrange("p (b k) -> p k b", k=KH)[:, kc, :],
                            start=(kc == 0), stop=(kc == KH - 1))
            last.then_inc(modc_mm, 1)
            pe.wait_ge(norm1.xn_done, TT)
            turn(norm1, chunk(0), 0, tp)
            pe.wait_ge(norm1.h_done, 1)
            turn(norm1, chunk(0), 1, tp)
            pe.wait_ge(sq_in, 4 * 16)
            pe.wait_ge(modc_done, 4)
            for w in range(4):
                for kc in range(KH):
                    for oc in range(KH):
                        last = nc.tensor.transpose(mm[w][:, kc * H + oc * P:kc * H + (oc + 1) * P],
                                                   w_nat[:, w, oc, kc * P:(kc + 1) * P], ident[:, :])
                last.then_inc(w_turned, 1)
            pe.wait_ge(gw_in, 16)
            for kc in range(KH):
                last = nc.tensor.transpose(cb[:, kc * E:(kc + 1) * E], gw[:, kc * P:(kc + 1) * P],
                                           ident[0:E, 0:E])
            last.then_inc(w_turned, 1)
            pe.wait_ge(wt_done, 4)
            pe.wait_ge(init_done, 1)
            project(chunk(0), first=True)
            for b in range(B):
                if b >= 2:
                    pe.wait_ge(gates_step, 8 * (b - 1))
                for g, q in enumerate((2, 5)):
                    for kc in range(KH):
                        last = nc.tensor.matmul(
                            yo[b % 2][:, g * H:(g + 1) * H],
                            condT[:, 2 * b + kc:2 * b + kc + 1].to_broadcast([P, P]),
                            wmod_sb[:, kc, q * H:(q + 1) * H], start=(kc == 0), stop=(kc == KH - 1))
                last.then_inc(gates_mm, 1)
            turn1(chunk(1), 0)
            turn1(chunk(1), 1)
            pe.wait_ge(bias_done, 2)
            pe.wait_ge(wog_done, B)
            output(chunk(0))
            project_after_first = chunk(1)
            pe.wait_ge(kvr_done, 3 * KH)
            project(project_after_first, first=True)
            pe.wait_ge(gwt_done, 1)
            turn2(chunk(0))
            logits(chunk(0))
            turn_comb(chunk(0))
            pe.wait_ge(up_lo_done, 4)
            pe.wait_ge(wdg_done, B * NB)
            with pe.Fori(0, 3) as i:
                for offset in (1, 2):
                    step(*(chunk_in_loop(i, offset + d) for d in (-1, 0, 1)))
            step(chunk(NC - 2), chunk(NC - 1), None)
            for e in range(NB):
                up(chunk(NC - 1), e, after_up=True)
            down(chunk(NC - 1), (0, 1), last_chunk=True)
            down(chunk(NC - 1), (2, 3), last_chunk=True)

        @block.vector
        def _(ve):
            def stats(norm, src, c, ready):
                wait(ve, norm.rstd_done, c.n)
                wait(ve, ready[0], ready[1])
                for t in range(TT):
                    nc.vector.bn_stats(norm.stats[:, t, :], src[:, t, :]).then_inc(norm.bn_done, 1)
                ve.wait_ge(norm.bn_done, TT * (c.n + 1))
                nc.vector.memset(pace[:, :], 0.0)
                for t in range(TT):
                    nc.vector.bn_aggr(norm.mv[:, t, :], norm.stats[:, t, :]).then_inc(norm.mv_done, 1)

            def stats1(c):
                stats(norm1, x_in[c.half], c, (x_loaded[c.half], 16 * (c.batch + 1)))

            def mix(c):
                h = hT[c.half]
                wait(ve, kvr_mm, 3 * KH * c.n)
                for kc in range(KH):
                    ve.wait_ge(norm1.h_done, KH * c.n + kc + 1)
                    nc.vector.tensor_tensor(diff[:, kc, :], h[:, kc, 1:CH + 1], h[:, kc, 0:CH], ALU.subtract
                                            ).then_inc(diff_done, 1)
                for w in range(3):
                    for kc in range(KH):
                        if w == 0:
                            ve.wait_ge(diff_done, KH * c.n + kc + 1)
                        nc.vector.scalar_tensor_tensor(
                            out=mixed[:, w, kc, :], in0=diff[:, kc, :], scalar=mix_cols[w][:, kc:kc + 1],
                            in1=h[:, kc, 0:CH], op0=ALU.mult, op1=ALU.add).then_inc(mixed_done, 1)

            def scan_max(c):
                st = state
                if c.half:
                    nc.vector.tensor_copy(st[:, 0, :, 0:1], st[:, 0, :, CH:CH + 1]).then_inc(seed_done, 1)
                else:
                    nc.vector.memset(st[:, 0, :, 0:1], START).then_inc(seed_done, 1)
                ve.wait_ge(seed_done, 2 * c.n + 1)
                for h in range(KH):
                    ve.wait_ge(kvr_done, 3 * KH * c.n + h + 1)
                    nc.vector.tensor_tensor_scan(st[:, 0, h, 1:CH + 1], decay[:, h:h + 1].to_broadcast([P, CH]),
                                                 kvr[:, K, h, :], st[:, 0, h, 0:1], ALU.add, ALU.max
                                                 ).then_inc(pp_done, 1)
                for h in range(KH):
                    before, after, k = st[:, 0, h, 0:CH], st[:, 0, h, 1:CH + 1], kvr[:, K, h, :]
                    ve.wait_ge(pp_done, KH * c.n + h + 1)
                    nc.vector.scalar_tensor_tensor(out=arg[:, 0, h, :], in0=before, scalar=decay[:, h:h + 1],
                                                   in1=after, op0=ALU.add, op1=ALU.subtract
                                                   ).then_inc(arg_done, 1)
                    nc.vector.tensor_tensor(arg[:, 1, h, :], k, after, ALU.subtract).then_inc(arg_done, 1)
                    nc.vector.scalar_tensor_tensor(out=tmp[:, h, :], in0=k, scalar=col["tf"][:, h:h + 1],
                                                   in1=before, op0=ALU.add, op1=ALU.subtract
                                                   ).then_inc(arg_done, 1)

            def scan_sums(c):
                st = state
                if c.half:
                    nc.vector.tensor_copy(st[:, 1:3, :, 0:1], st[:, 1:3, :, CH:CH + 1]
                                          ).then_inc(seed_done, 1)
                else:
                    nc.vector.memset(st[:, 1:3, :, 0:1], 0.0).then_inc(seed_done, 1)
                for h in range(KH):
                    ve.wait_ge(kvr_done, 3 * KH * c.n + KH + h + 1)
                    ve.wait_ge(exp_done, 4 * (KH * c.n + h) + 2)
                    nc.vector.tensor_tensor(ev[:, h, :], arg[:, 1, h, :], kvr[:, V, h, :], ALU.mult
                                            ).then_inc(ev_done, 1)
                ve.wait_ge(seed_done, 2 * c.n + 2)
                for h in range(KH):
                    nc.vector.tensor_tensor_scan(st[:, 2, h, 1:CH + 1], arg[:, 0, h, :], arg[:, 1, h, :],
                                                 st[:, 2, h, 0:1], ALU.mult, ALU.add).then_inc(aabb_done, 1)
                    ve.wait_ge(ev_done, KH * c.n + h + 1)
                    nc.vector.tensor_tensor_scan(st[:, 1, h, 1:CH + 1], arg[:, 0, h, :], ev[:, h, :],
                                                 st[:, 1, h, 0:1], ALU.mult, ALU.add).then_inc(aabb_done, 1)
                for h in range(KH):
                    e1, e2 = arg[:, 2, h, :], arg[:, 3, h, :]
                    ve.wait_ge(exp_done, 4 * (KH * c.n + h) + 4)
                    ve.wait_ge(aabb_done, 2 * (KH * c.n + h) + 2)
                    nc.vector.tensor_tensor(den[:, h, :], e1, st[:, 2, h, 0:CH], ALU.mult
                                            ).then_inc(part_done, 1)
                    nc.vector.tensor_tensor(num[:, h, :], e1, st[:, 1, h, 0:CH], ALU.mult
                                            ).then_inc(part_done, 1)
                    ve.wait_ge(part_done, 3 * (KH * c.n + h) + 1)
                    nc.vector.tensor_tensor(den[:, h, :], den[:, h, :], e2, ALU.add).then_inc(den_done, 1)
                    nc.vector.tensor_tensor(ev[:, h, :], e2, kvr[:, V, h, :], ALU.mult
                                            ).then_inc(part_done, 1)
                for h in range(KH):
                    ve.wait_ge(part_done, 3 * (KH * c.n + h + 1))
                    nc.vector.tensor_tensor(num[:, h, :], num[:, h, :], ev[:, h, :], ALU.add
                                            ).then_inc(num_done, 1)

            def divide(c, h, n):
                if n == 0:
                    ve.wait_ge(num_done, KH * c.n + h + 1)
                    ve.wait_ge(rec_done, KH * c.n + h + 1)
                    nc.vector.tensor_tensor(ev[:, h, :], num[:, h, :], rec[:, h, :], ALU.mult
                                            ).then_inc(newton_done, 1)
                elif n == 1:
                    nc.vector.tensor_tensor(tmp[:, h, :], den[:, h, :], rec[:, h, :], ALU.mult
                                            ).then_inc(newton_done, 1)
                elif n == 2:
                    ve.wait_ge(newton_done, 3 * KH * c.n + KH + h + 1)
                    nc.vector.scalar_tensor_tensor(out=num[:, h, :], in0=tmp[:, h, :], scalar=2.0,
                                                   in1=ev[:, h, :], op0=ALU.subtract, op1=ALU.mult
                                                   ).then_inc(newton_done, 1)
                else:
                    ve.wait_ge(newton_done, 3 * KH * c.n + 2 * KH + h + 1)
                    ve.wait_ge(sgm_done, KH * c.n + h + 1)
                    nc.vector.scalar_tensor_tensor(out=rw[:, h, :], in0=sgm[:, h, :], scalar=1.0,
                                                   in1=num[:, h, :], op0=ALU.add, op1=ALU.mult
                                                   ).then_inc(rw_done, 1)

            def residual1(c):
                ve.wait_ge(stored[c.half], 16 * (c.batch + 1))
                for k in range(2):
                    ve.wait_ge(wo_mm, 2 * c.n + k + 1)
                    nc.vector.tensor_tensor(
                        x1[c.half][:, 2 * k:2 * k + 2, :], yo[k][:, :].rearrange("p (t h) -> p t h", t=2),
                        x_in[c.half][:, 2 * k:2 * k + 2, :], ALU.add).then_inc(x1_done, 1)

            def residual2(c):
                for k in range(2):
                    ve.wait_ge(down_mm, 2 * c.n + k + 1)
                    nc.vector.tensor_tensor(
                        x1[c.half][:, 2 * k:2 * k + 2, :], yo[k][:, :].rearrange("p (t h) -> p t h", t=2),
                        x1[c.half][:, 2 * k:2 * k + 2, :], ALU.add).then_inc(x2_done, 1)

            def low_part(c):
                for kc in range(KH):
                    ve.wait_ge(norm2.h_done, KH * c.n + kc + 1)
                    nc.vector.tensor_tensor(h2_l[:, kc, :], h2[:, kc, :], h2_h[:, kc, :].bitcast(F32),
                                            ALU.subtract).then_inc(h2lo_done, 1)

            def route(c):
                lg = tp[:, 0:TT * E].rearrange("p (t e) -> p t e", e=E)
                eq, pr, m1, l2, m2, w1m, w2m, both = (rt[:, n, :, :] for n in range(8))
                v1, v2, gap, ex, p1, s, w1, w2 = (r1[:, n, :] for n in range(8))
                wide = lambda v: v.unsqueeze(2).to_broadcast([P, TT, E])
                at = [0]

                def then(ins):
                    at[0] += 1
                    ins.then_inc(route_step, 1)
                    ve.wait_ge(route_step, ROUTE_STEPS * c.n + at[0])

                V = nc.vector
                ve.wait_ge(logits_mm, c.n + 1)
                then(V.tensor_reduce(v1, lg, AX.X, ALU.max))
                then(V.tensor_tensor(eq, lg, wide(v1), ALU.is_equal))
                then(V.tensor_tensor(pr, eq, prio[:, :, :], ALU.mult))
                then(V.tensor_reduce(s, pr, AX.X, ALU.max))
                then(V.tensor_tensor(m1, prio[:, :, :], wide(s), ALU.is_equal))
                then(V.scalar_tensor_tensor(out=l2, in0=m1, scalar=-3e38, in1=lg, op0=ALU.mult, op1=ALU.add))
                then(V.tensor_reduce(v2, l2, AX.X, ALU.max))
                V.tensor_tensor(gap, v2, v1, ALU.subtract).then_inc(gap_done, 1)
                then(V.tensor_tensor(eq, l2, wide(v2), ALU.is_equal))
                then(V.tensor_tensor(pr, eq, prio[:, :, :], ALU.mult))
                then(V.tensor_reduce(s, pr, AX.X, ALU.max))
                then(V.tensor_tensor(m2, prio[:, :, :], wide(s), ALU.is_equal))
                ve.wait_ge(gap_exp, c.n + 1)
                then(V.tensor_scalar(p1, ex, 1.0, None, ALU.add))
                then(V.reciprocal(w1, p1))
                then(V.tensor_tensor(w2, ex, w1, ALU.mult))
                then(V.tensor_tensor(w1m, m1, wide(w1), ALU.mult))
                then(V.tensor_tensor(w2m, m2, wide(w2), ALU.mult))
                then(V.tensor_tensor(both, w1m, w2m, ALU.add))
                V.tensor_copy(comb[:, :, 0:E], both).then_inc(route_step, 1)
                ve.wait_ge(route_step, ROUTE_STEPS * c.n + ROUTE_STEPS)
                V.tensor_tensor(comb[:, :, E:2 * E], both, comb[:, :, 0:E].bitcast(F32), ALU.subtract
                                ).then_inc(comb_done, 1)

            def gate_up(c, e):
                ve.wait_ge(silu_done, NB * c.n + e + 1)
                ve.wait_ge(up_mm, 2 * (NB * c.n + e) + 2)
                dst = act if e == NP else sg
                nc.vector.tensor_tensor(dst[:, e, :], mm[(7 + 2 * e) % 4][:, :], sg[:, e, :], ALU.mult
                                        ).then_inc(prod_done, 1)

            def weigh(c, e):
                ve.wait_ge(comb_mm, NP * c.n + e + 1)
                ve.wait_ge(prod_done, NB * c.n + e + 1)
                nc.vector.tensor_tensor(act[:, e, :], cb[:, :], sg[:, e, :], ALU.mult).then_inc(act_done, 1)

            def step(prev, cur, nxt):
                if nxt:
                    stats1(nxt)
                for n in range(4):
                    for h in range(KH):
                        divide(cur, h, n)
                    if prev:
                        gate_up(prev, n)
                        weigh(prev, n)
                if prev:
                    gate_up(prev, NP)
                if nxt:
                    mix(nxt)
                residual1(cur)
                stats(norm2, x1[cur.half], cur, (x1_done, 2 * (cur.n + 1)))
                if nxt:
                    scan_max(nxt)
                low_part(cur)
                route(cur)
                if nxt:
                    scan_sums(nxt)
                if prev:
                    residual2(prev)

            for e in range(E):
                nc.vector.memset(prio[:, :, e], float(E - e))
            nc.vector.memset(hT[0][:, :, 0:1], 0.0)
            nc.vector.memset(gmag[:, 0, 0, 0:P], 1.0).then_inc(bias_step, 1)
            nc.vector.memset(bias_r[:, :, :].bitcast(F32), 0.0).then_inc(bias_step, 1)
            ve.wait_ge(bias_step, 2)
            nc.vector.tensor_copy(ones_r[:, :], gmag[:, 0, 0, 0:P]).then_inc(bias_step, 1)
            ve.wait_ge(sel_done, 2)
            nc.vector.tensor_copy(sel[:, :, :], sel_f[:, :, :]).then_inc(init_done, 1)
            ve.wait_ge(cols_turned, 1)
            nc.vector.tensor_copy(cols[:, :], mm[0][:, 0:24]).then_inc(cols_done, 1)
            stats1(chunk(0))
            ve.wait_ge(modc_mm, 1)
            for n in range(4):
                nc.vector.tensor_scalar(modc[:, n, :, :],
                                        mm[1][:, n * KH * B:(n + 1) * KH * B].rearrange("p (k b) -> p k b", b=B),
                                        float(n % 2), None, ALU.add).then_inc(modc_done, 1)
            ve.wait_ge(decay_done, 1)
            nc.vector.tensor_scalar(decay[:, :], decay[:, :], -1.0, None, ALU.mult).then_inc(decay_done, 1)
            mix(chunk(0))
            ve.wait_ge(decay_done, 2)
            scan_max(chunk(0))
            scan_sums(chunk(0))
            stats1(chunk(1))
            ve.wait_ge(bias_step, 3)
            for b in range(B):
                ve.wait_ge(gates_mm, b + 1)
                raw = yo[b % 2][:, :].rearrange("p (g h) -> p g h", g=2)
                for g, dst in enumerate((ga, gb)):
                    nc.vector.tensor_scalar(dst[:, b, :], raw[:, g, :], 0.0, 2.0, ALU.is_ge, ALU.mult
                                            ).then_inc(gates_step, 1)
                for g, dst in enumerate((ga, gb)):
                    ve.wait_ge(gates_step, 8 * b + g + 1)
                    nc.vector.scalar_tensor_tensor(out=gmag[:, b % 2, g, :], in0=dst[:, b, :], scalar=1.0,
                                                   in1=raw[:, g, :], op0=ALU.subtract, op1=ALU.mult
                                                   ).then_inc(gates_step, 1)
                for g in range(2):
                    ve.wait_ge(gates_step, 8 * b + g + 3)
                    nc.vector.tensor_scalar(gmag[:, b % 2, g, :], gmag[:, b % 2, g, :], 0.25, None, ALU.max
                                            ).then_inc(gates_step, 1)
                for g, dst in enumerate((ga, gb)):
                    ve.wait_ge(gates_step, 8 * b + g + 5)
                    nc.vector.scalar_tensor_tensor(out=dst[:, b, :], in0=dst[:, b, :], scalar=1.0,
                                                   in1=gmag[:, b % 2, g, :], op0=ALU.subtract, op1=ALU.mult
                                                   ).then_inc(gates_step, 1)
            ve.wait_ge(gates_step, 8 * B)
            ve.wait_ge(bo_in, 16)
            ve.wait_ge(wt_done, 4)
            for b in range(B):
                nc.vector.tensor_tensor(WoG[:, b, :, :], WT[:, O, :, :],
                                        ga[:, b, :].unsqueeze(1).to_broadcast([P, KH, H]), ALU.mult
                                        ).then_inc(wog_done, 1)
            ve.wait_ge(wog_done, B)
            nc.vector.tensor_tensor(gabo[:, :, :], ga[:, :, :], bo_b[:, :].unsqueeze(1).to_broadcast([P, B, H]),
                                    ALU.mult).then_inc(gates_done, 1)
            ve.wait_ge(gates_done, 1)
            nc.vector.tensor_copy(bias_r[0:1, :, :], gabo[0:1, :, :]).then_inc(bias_done, 1)
            nc.vector.tensor_copy(bias_r[32:33, :, :], gabo[32:33, :, :]).then_inc(bias_step, 1)
            ve.wait_ge(bias_step, 4)
            nc.vector.tensor_tensor(bias_r[32:33, :, :], gabo[32:33, :, :], bias_r[32:33, :, :].bitcast(F32),
                                    ALU.subtract).then_inc(bias_done, 1)
            for n in range(4):
                for h in range(KH):
                    divide(chunk(0), h, n)
            mix(chunk(1))
            residual1(chunk(0))
            stats(norm2, x1[0], chunk(0), (x1_done, 2))
            scan_max(chunk(1))
            low_part(chunk(0))
            route(chunk(0))
            scan_sums(chunk(1))
            with ve.Fori(0, 3) as i:
                for offset in (1, 2):
                    step(*(chunk_in_loop(i, offset + d) for d in (-1, 0, 1)))
            last = chunk(NC - 1)
            step(chunk(NC - 2), last, None)
            for e in range(NB):
                gate_up(last, e)
                if e < NP:
                    weigh(last, e)
            residual2(last)


_INS = ['L0_attn_x', 'L0_attn_Wk', 'L0_attn_bk', 'L0_attn_Wv', 'L0_attn_bv', 'L0_attn_Wr', 'L0_attn_br',
        'L0_attn_Wo', 'L0_attn_bo', 'L0_attn_tmk', 'L0_attn_tmv', 'L0_attn_tmr', 'L0_attn_time_decay',
        'L0_attn_time_first', 'L0_ffn_gate_w', 'L0_ffn_Wg', 'L0_ffn_Wu', 'L0_ffn_Wd', 'L0_ffn_sWg',
        'L0_ffn_sWu', 'L0_ffn_sWd', 'L0_c', 'L0_wmod']
_ROWS = {'L0_attn_bk', 'L0_attn_bv', 'L0_attn_br', 'L0_attn_tmk', 'L0_attn_tmv', 'L0_attn_tmr',
         'L0_attn_time_decay', 'L0_attn_time_first', 'L0_c'}


def kernel(**inputs):
    import numpy as _np
    import concourse.bacc as _bacc
    from concourse import mybir as _mybir
    from concourse.bass_utils import run_bass_kernel_spmd as _run

    nc = _bacc.Bacc("TRN2", target_bir_lowering=False, num_devices=1)
    arrays, args = {}, []
    for name in _INS:
        a = _np.ascontiguousarray(inputs[name])
        if name in _ROWS:
            a = a.reshape(-1, P)
        arrays[f"in_{name}_dram"] = a
        args.append(nc.dram_tensor(f"in_{name}_dram", a.shape, _mybir.dt.from_np(a.dtype), kind="ExternalInput").ap())
    out = nc.dram_tensor("out_0_dram", (B, T, H), F32, kind="ExternalOutput").ap()
    adaln_rwkv_moe(nc, *args, out)
    r = _run(nc, [arrays], core_ids=[0])
    return r.results[0]["out_0_dram"]
```

```python
from collections import namedtuple
from contextlib import ExitStack

import concourse.bass as bass
from concourse import mybir

ALU = mybir.AluOpType
ACT = mybir.ActivationFunctionType
AX = mybir.AxisListType
F32 = mybir.dt.float32
F32R = mybir.dt.float32r

P = 128
B, T, H = 4, 1024, 256
KH = H // P
CH = 512
TT = CH // P
NC = B * T // CH
E, M = 8, 64
NP = E * M // P
NB = NP + 1
EPS = 1e-5
START = -1e30
K, V, R, O = range(4)

EXP_SET = "natural_log_exp_and_others"
SILU_SET = "silu_and_others"

Chunk = namedtuple("Chunk", "n batch half")


def chunk(n):
    return Chunk(n, n // 2, n % 2)


def chunk_in_loop(i, offset):
    return Chunk(2 * i + offset, i + offset // 2, offset % 2)


def adaln_rwkv_moe(nc, x, Wk, bk, Wv, bv, Wr, br, Wo, bo, tmk, tmv, tmr, time_decay, time_first,
                   gate_w, Wg, Wu, Wd, sWg, sWu, sWd, cond, wmod, out):
    x_chunks = x.rearrange("b (g t p) h -> (b g) p t h", t=TT, p=P)
    out_chunks = out.rearrange("b (g t p) h -> (b g) p t h", t=TT, p=P)

    with ExitStack() as ctx:
        def sb(name, shape, dt=F32):
            return ctx.enter_context(nc.sbuf_tensor(name, shape, dt))

        def sem(name):
            return ctx.enter_context(nc.semaphore(name))

        ident = sb("ident", [P, P])
        ones_r = sb("ones_r", [P, P], F32R)
        sel = sb("sel", [2 * E, NP, P], F32R)
        prio = sb("prio", [P, TT, E])
        small = sb("small", [P, 3, TT])
        rows = sb("rows", [24, P])
        cols = sb("cols", [P, 24])
        condT = sb("condT", [P, 2 * B])
        decay = sb("decay", [P, KH])
        modc = sb("modc", [P, 4, KH, B])
        gb = sb("gb", [P, B, H])
        bo_b = sb("bo_b", [P, H])
        pace = sb("pace", [P, 1])
        mod1 = sb("mod1", [P, 2, KH])
        mod2 = sb("mod2", [P, 2, KH])
        bias_r = sb("bias_r", [P, B, H], F32R)
        WT = sb("WT", [P, 4, KH, H])
        WoG = sb("WoG", [P, B, KH, H])
        gw = sb("gw", [E, H])
        gwT = sb("gwT", [P, KH, E])
        gw_hl = sb("gw_hl", [P, KH, 2 * E], F32R)
        rest = sb("rest", [P, 3 * KH])
        w_up_h = sb("w_up_h", [P, KH, 2, NB * P], F32R)
        w_up_l = sb("w_up_l", [P, KH, 2, NB * P], F32R)
        WdG = sb("WdG", [P, B, NB, H])

        x_in = [sb(f"x_in{h}", [P, TT, H]) for h in range(2)]
        hT = [sb(f"hT{h}", [P, KH, CH + 1]) for h in range(2)]
        mixed = sb("mixed", [P, 3, KH, CH])
        kvr = sb("kvr", [P, 3, KH, CH])
        state = sb("state", [P, 3, KH, CH + 1])
        arg = sb("arg", [P, 4, KH, CH])
        ev = sb("ev", [P, KH, CH])
        tmp = sb("tmp", [P, KH, CH])
        h2_h = sb("h2_h", [P, KH, CH], F32R)
        h2_l = sb("h2_l", [P, KH, CH], F32R)
        rt = sb("rt", [P, 9, TT, E])
        r1 = sb("r1", [P, 8, TT])
        comb = sb("comb", [P, TT, 2 * E], F32R)
        combT = sb("combT", [2 * E, CH], F32R)
        pool_x = sb("pool_x", [P, 3 * TT * H])
        pool_n = sb("pool_n", [P, 2 * KH * CH])
        pool_g = sb("pool_g", [P, NB * CH])
        pool_a = sb("pool_a", [P, NB * CH])
        wmod_sb = pool_x[:, :].rearrange("p (k q) -> p k q", k=KH)
        x1 = [pool_x[:, h * TT * H:(h + 1) * TT * H].rearrange("p (t h) -> p t h", t=TT) for h in range(2)]
        h2 = pool_x[:, 2 * TT * H:].rearrange("p (k n) -> p k n", k=KH)
        w_nat = pool_n[:, :].rearrange("p (w a h) -> p w a h", w=4, a=KH)
        num = pool_n[:, 0:KH * CH].rearrange("p (k n) -> p k n", k=KH)
        den = pool_n[:, KH * CH:].rearrange("p (k n) -> p k n", k=KH)
        w_up = pool_g[:, :].rearrange("p (k g n) -> p k g n", k=KH, g=2)
        sg = pool_g[:, :].rearrange("p (e n) -> p e n", e=NB)
        w_dn = pool_a[:, 0:NB * H].rearrange("p (e h) -> p e h", e=NB)
        ga = pool_a[:, NB * H:NB * H + B * H].rearrange("p (b h) -> p b h", b=B)
        act = pool_a[:, :].rearrange("p (e n) -> p e n", e=NB)
        sel_f = tmp[0:2 * E, 0, :].rearrange("p (i n) -> p i n", i=NP)
        rec = arg[:, 0, :, :]
        sgm = kvr[:, R, :, :]
        rw = num

        mm = [ctx.enter_context(nc.psum_tensor(f"mm{i}", [P, CH], F32)) for i in range(4)]
        yo = [ctx.enter_context(nc.psum_tensor(f"yo{i}", [P, CH], F32)) for i in range(2)]
        tp = ctx.enter_context(nc.psum_tensor("tp", [P, CH], F32))
        cb = ctx.enter_context(nc.psum_tensor("cb", [P, CH], F32))

        comb_bank = {1: cb, 2: cb, 3: cb, 4: tp}

        class Norm:

            def __init__(self, name):
                self.stats = sb(f"{name}_stats", [P, TT, 6])
                self.mv = sb(f"{name}_mv", [P, TT, 2])
                self.ve = sb(f"{name}_ve", [P, TT])
                self.rstd = sb(f"{name}_rstd", [P, TT])
                self.mr = sb(f"{name}_mr", [P, TT])
                self.shift = sb(f"{name}_shift", [P, TT])
                self.xn = sb(f"{name}_xn", [P, TT, H])
                self.bn_done = sem(f"{name}_bn_done")
                self.mv_done = sem(f"{name}_mv_done")
                self.pool_step = sem(f"{name}_pool_step")
                self.rstd_done = sem(f"{name}_rstd_done")
                self.xn_done = sem(f"{name}_xn_done")
                self.turned = sem(f"{name}_turned")
                self.h_done = sem(f"{name}_h_done")

        norm1, norm2 = Norm("n1"), Norm("n2")
        gabo = ga
        gmag = norm2.xn[:, :, :].rearrange("p (b g) h -> p b g h", b=2)

        rows_in, cond_in, sq_in, up_in, dn_in, bo_in, gw_in = (
            sem(n) for n in ("rows_in", "cond_in", "sq_in", "up_in", "dn_in", "bo_in", "gw_in"))
        consts_done, ident_done, sel_done = sem("consts_done"), sem("ident_done"), sem("sel_done")
        init_done = sem("init_done")
        cols_turned, cols_done, cond_done, decay_done, rest_done = (
            sem(n) for n in ("cols_turned", "cols_done", "cond_done", "decay_done", "rest_done"))
        modc_mm, modc_done, gates_mm, gates_step, gates_done = (
            sem(n) for n in ("modc_mm", "modc_done", "gates_mm", "gates_step", "gates_done"))
        bias_step, bias_done = sem("bias_step"), sem("bias_done")
        w_turned, wt_done, wog_done, gwt_done = (
            sem(n) for n in ("w_turned", "wt_done", "wog_done", "gwt_done"))
        up_hi_done, up_lo_done, wdg_done = sem("up_hi_done"), sem("up_lo_done"), sem("wdg_done")
        x_loaded = [sem(f"x_loaded{h}") for h in range(2)]
        stored = [sem(f"stored{h}") for h in range(2)]
        part_mixed = sem("part_mixed")
        mixed_done = sem("mixed_done")
        kvr_mm = sem("kvr_mm")
        kvr_done = sem("kvr_done")
        seed_done = sem("seed_done")
        pp_done = sem("pp_done")
        arg_done = sem("arg_done")
        relu_done = sem("relu_done")
        exp_done = sem("exp_done")
        ev_done = sem("ev_done")
        bb_done = sem("bb_done")
        aa_done = sem("aa_done")
        part_done = sem("part_done")
        num_done = sem("num_done")
        den_done = sem("den_done")
        ln_done = sem("ln_done")
        rec_done = sem("rec_done")
        newton_done = sem("newton_done")
        sgm_done = sem("sgm_done")
        rw_done = sem("rw_done")
        wo_mm = sem("wo_mm")
        x1_done = sem("x1_done")
        h2lo_done = sem("h2lo_done")
        logits_mm = sem("logits_mm")
        route_step = sem("route_step")
        gap_done = sem("gap_done")
        gap_exp = sem("gap_exp")
        comb_done = sem("comb_done")
        comb_turned = sem("comb_turned")
        combT_done = sem("combT_done")
        comb_mm = sem("comb_mm")
        up_mm = sem("up_mm")
        silu_done = sem("silu_done")
        prod_done = sem("prod_done")
        act_done = sem("act_done")
        down_mm = sem("down_mm")
        x2_done = sem("x2_done")

        col = {n: cols[:, 2 * B + KH * i:2 * B + KH * (i + 1)]
               for i, n in enumerate(("tmk", "tmv", "tmr", "bk", "bv", "br", "td", "tf"))}
        mix_cols = (col["tmk"], col["tmv"], col["tmr"])
        bias_cols = (col["bk"], col["bv"], col["br"])
        mod1_done, mod2_done = sem("mod1_done"), sem("mod2_done")
        ROUTE_STEPS = 19

        block = ctx.enter_context(nc.Block())

        def wait(eng, s, value):
            if not (isinstance(value, int) and value <= 0):
                eng.wait_ge(s, value)

        @block.sync
        def _(sp):
            def load(c, first=False):
                if not first:
                    wait(sp, x1_done, 2 * (c.n - 1))
                sp.dma_start(x_in[c.half][:, :, :], x_chunks[c.n]).then_inc(x_loaded[c.half], 16)

            def store(c):
                wait(sp, x2_done, 2 * (c.n + 1))
                sp.dma_start(out_chunks[c.n], x1[c.half][:, :, :]).then_inc(stored[c.half], 16)

            load(chunk(0), first=True)
            for h in range(2):
                sp.sem_inc(stored[h], 16)
            for kc in range(KH):
                sp.dma_start(wmod_sb[:, kc, :], wmod[kc * P:(kc + 1) * P, :]).then_inc(cond_in, 16)
            load(chunk(1), first=True)
            sp.dma_start(bo_b[:, :], bo.rearrange("(a h) -> a h", a=1).to_broadcast([P, H])
                         ).then_inc(bo_in, 16)
            for kc in range(KH):
                sp.dma_start(w_up[:, kc, 0, P:].rearrange("p (e m) -> p e m", m=M),
                             Wg[:, kc * P:(kc + 1) * P, :].rearrange("e p m -> p e m")).then_inc(up_in, 16)
                sp.dma_start(w_up[:, kc, 0, 0:P], sWg[kc * P:(kc + 1) * P, :]).then_inc(up_in, 16)
            sp.dma_start(w_dn[:, 1:, :], Wd.rearrange("(i e) m h -> (e m) i h", e=2)).then_inc(dn_in, 16)
            sp.dma_start(w_dn[:, 0, :], sWd).then_inc(dn_in, 16)
            load(chunk(2))
            with sp.Fori(0, 2) as i:
                for offset in (0, 1):
                    load(chunk_in_loop(i, offset + 3))
                    store(chunk_in_loop(i, offset))
            load(chunk(NC - 1))
            for n in range(4, NC):
                store(chunk(n))
            for h in range(2):
                sp.wait_ge(stored[h], 16 * (NC // 2 + 1))

        @block.gpsimd
        def _(pool):
            nc.gpsimd.memset(ident[:, :], 0.0).then_inc(consts_done, 1)
            nc.gpsimd.memset(sel_f[:, :, :], 0.0).then_inc(consts_done, 1)
            nc.gpsimd.memset(small[:, 0, :], EPS).then_inc(consts_done, 1)
            nc.gpsimd.memset(small[:, 1, :], -0.5).then_inc(consts_done, 1)
            nc.gpsimd.memset(small[:, 2, :], 0.0).then_inc(consts_done, 1)
            pool.wait_ge(consts_done, 5)
            nc.gpsimd.affine_select(out=ident[:, :], in_=ident[:, :], compare_op=ALU.not_equal, fill=1.0,
                                    base=0, pattern=[[-1, P]], channel_multiplier=1).then_inc(ident_done, 1)
            for part in range(2):
                pool.wait_ge(sel_done, part) if part else None
                nc.gpsimd.affine_select(
                    out=sel_f[:, :, :].rearrange("p i (e m) -> p i e m", m=M),
                    in_=sel_f[:, :, :].rearrange("p i (e m) -> p i e m", m=M),
                    compare_op=ALU.not_equal, fill=1.0, base=-E * part,
                    pattern=[[-2, NP], [-1, 2], [0, M]], channel_multiplier=1).then_inc(sel_done, 1)

            def rstd(norm, c):
                wait(pool, norm.mv_done, TT * (c.n + 1))
                wait(pool, norm.xn_done, TT * c.n)
                nc.gpsimd.tensor_tensor(norm.ve[:, :], norm.mv[:, :, 1], small[:, 0, :], ALU.add
                                        ).then_inc(norm.pool_step, 1)
                pool.wait_ge(norm.pool_step, 3 * c.n + 1)
                nc.gpsimd.tensor_tensor(norm.rstd[:, :], norm.ve[:, :], small[:, 1, :], ALU.pow
                                        ).then_inc(norm.pool_step, 1)
                pool.wait_ge(norm.pool_step, 3 * c.n + 2)
                nc.gpsimd.tensor_tensor(norm.mr[:, :], norm.mv[:, :, 0], norm.rstd[:, :], ALU.mult
                                        ).then_inc(norm.pool_step, 1)
                pool.wait_ge(norm.pool_step, 3 * c.n + 3)
                nc.gpsimd.tensor_tensor(norm.shift[:, :], small[:, 2, :], norm.mr[:, :], ALU.subtract
                                        ).then_inc(norm.rstd_done, 1)

            rstd(norm1, chunk(0))
            pool.wait_ge(up_hi_done, 4)
            for kc in range(KH):
                for gu in range(2):
                    nc.gpsimd.tensor_tensor(w_up_l[:, kc, gu, :], w_up[:, kc, gu, :],
                                            w_up_h[:, kc, gu, :].bitcast(F32), ALU.subtract
                                            ).then_inc(up_lo_done, 1)
            rstd(norm1, chunk(1))
            pool.wait_ge(dn_in, 32)
            pool.wait_ge(gates_step, 8 * B)
            for b in range(B):
                for e in range(NB):
                    nc.gpsimd.tensor_tensor(WdG[:, b, e, :], w_dn[:, e, :], gb[:, b, :], ALU.mult
                                            ).then_inc(wdg_done, 1)
            rstd(norm2, chunk(0))
            with pool.Fori(0, 3) as i:
                for offset in (1, 2):
                    rstd(norm1, chunk_in_loop(i, offset + 1))
                    rstd(norm2, chunk_in_loop(i, offset))
            rstd(norm2, chunk(NC - 1))

        @block.scalar
        def _(ac):
            def normalise(norm, src, c, pick_mod=True):
                wait(ac, norm.rstd_done, c.n + 1)
                wait(ac, norm.turned, KH * c.n)
                for t in range(TT):
                    nc.scalar.activation(norm.xn[:, t, :], src[:, t, :], ACT.Identity,
                                         bias=norm.shift[:, t:t + 1], scale=norm.rstd[:, t:t + 1]
                                         ).then_inc(norm.xn_done, 1)
                if pick_mod:
                    pick(norm, c)

            def pick(norm, c):
                if c.half == 0:
                    mod, first, done = (mod1, 0, mod1_done) if norm is norm1 else (mod2, 2, mod2_done)
                    nc.scalar.activation(mod[:, :, :], modc[:, first:first + 2, :, bass.ds(c.batch, 1)]
                                         .rearrange("p q k b -> p q (k b)"), ACT.Identity).then_inc(done, 1)

            def affine1(c, kc):
                ac.wait_ge(norm1.turned, KH * c.n + kc + 1)
                wait(ac, mixed_done, 3 * KH * c.n)
                ac.wait_ge(mod1_done, c.batch + 1)
                scale, shift = mod1[:, 1, kc:kc + 1], mod1[:, 0, kc:kc + 1]
                last = nc.scalar.activation(hT[c.half][:, kc, 1:CH + 1], tp[:, :], ACT.Identity,
                                            bias=shift, scale=scale)
                if c.half == 0:
                    last = nc.scalar.activation(hT[1][:, kc, 0:1], tp[:, CH - 1:CH], ACT.Identity,
                                                bias=shift, scale=scale)
                last.then_inc(norm1.h_done, 1)

            def affine2(c, kc):
                src = (tp, cb)[kc]
                ac.wait_ge(mod2_done, c.batch + 1)
                ac.wait_ge(norm2.turned, KH * c.n + kc + 1)
                scale, shift = mod2[:, 1, kc:kc + 1], mod2[:, 0, kc:kc + 1]
                nc.scalar.activation(h2_h[:, kc, :], src[:, :], ACT.Identity, bias=shift, scale=scale)
                nc.scalar.activation(h2[:, kc, :], src[:, :], ACT.Identity, bias=shift, scale=scale
                                     ).then_inc(norm2.h_done, 1)

            def add_bias(c, j):
                w, kc = divmod(j, KH)
                ac.wait_ge(kvr_mm, 3 * KH * c.n + j + 1)
                nc.scalar.activation(kvr[:, w, kc, :], mm[j % 4][:, :], ACT.Identity,
                                     bias=bias_cols[w][:, kc:kc + 1]).then_inc(kvr_done, 1)

            def part_mix(c, w):
                if w == 0:
                    wait(ac, kvr_mm, 3 * KH * c.n)
                for kc in range(KH):
                    if w == 0:
                        ac.wait_ge(norm1.h_done, KH * c.n + kc + 1)
                    nc.scalar.activation(mixed[:, w, kc, :], hT[c.half][:, kc, 0:CH], ACT.Identity,
                                         scale=rest[:, KH * w + kc:KH * w + kc + 1]).then_inc(part_mixed, 1)

            def state_exponentials(c):
                for n, j in enumerate((1, 0)):
                    ac.wait_ge(arg_done, 5 * c.n + 2 + n)
                    nc.scalar.activation(arg[:, j, :, :], arg[:, j, :, :], ACT.Exp).then_inc(exp_done, 1)

            def output_exponentials(c):
                ac.wait_ge(arg_done, 5 * c.n + 5)
                for j, sign in ((2, 1.0), (3, -1.0)):
                    nc.scalar.activation(arg[:, j, :, :], tmp[:, :, :], ACT.Relu, scale=sign
                                         ).then_inc(relu_done, 1)
                for j in range(2):
                    ac.wait_ge(relu_done, 2 * c.n + j + 1)
                    nc.scalar.activation(arg[:, 2 + j, :, :], arg[:, 2 + j, :, :], ACT.Exp, scale=-1.0
                                         ).then_inc(exp_done, 1)

            def reciprocal_seed(c):
                ac.wait_ge(den_done, c.n + 1)
                nc.scalar.activation(rec, den, ACT.Ln).then_inc(ln_done, 1)
                ac.wait_ge(ln_done, c.n + 1)
                nc.scalar.activation(rec, rec, ACT.Exp, scale=-1.0).then_inc(rec_done, 1)

            def tanh_r(c):
                ac.wait_ge(kvr_done, 3 * KH * (c.n + 1))
                nc.scalar.activation(sgm, sgm, ACT.Tanh, scale=0.5).then_inc(sgm_done, 1)

            def silu(c, e):
                ac.wait_ge(up_mm, 2 * (NB * c.n + e) + 1)
                nc.scalar.activation(sg[:, e, :], mm[(6 + 2 * e) % 4][:, :], ACT.Silu).then_inc(silu_done, 1)

            def project_and_scan(c, cur=None):
                add_bias(c, 0)
                add_bias(c, 1)
                if cur:
                    affine2(cur, 0)
                add_bias(c, 2)
                add_bias(c, 3)
                state_exponentials(c)
                if cur:
                    affine2(cur, 1)
                output_exponentials(c)
                add_bias(c, 4)
                add_bias(c, 5)
                if cur:
                    gap_exponential(cur)
                reciprocal_seed(c)

            def gap_exponential(c):
                ac.wait_ge(gap_done, c.n + 1)
                nc.scalar.activation(r1[:, 3, :], r1[:, 2, :], ACT.Exp).then_inc(gap_exp, 1)

            def comb_out(c):
                ac.wait_ge(comb_turned, c.n + 1)
                nc.scalar.activation(combT[:, :], cb[0:2 * E, :], ACT.Identity).then_inc(combT_done, 1)

            def step(prev, cur, nxt):
                nc.scalar.preload_act_table_set(SILU_SET)
                tanh_r(cur)
                if prev:
                    silu(prev, 0)
                    silu(prev, 1)
                    comb_out(prev)
                if nxt:
                    normalise(norm1, x_in[nxt.half], nxt)
                if prev:
                    silu(prev, 2)
                    silu(prev, 3)
                if nxt:
                    affine1(nxt, 0)
                    affine1(nxt, 1)
                    for w in range(3):
                        part_mix(nxt, w)
                if prev:
                    silu(prev, 4)
                normalise(norm2, x1[cur.half], cur)
                nc.scalar.preload_act_table_set(EXP_SET)
                if nxt:
                    project_and_scan(nxt, cur)
                else:
                    affine2(cur, 0)
                    affine2(cur, 1)
                    gap_exponential(cur)

            for r0, src in ((0, cond), (8, tmk), (10, tmv), (12, tmr), (14, bk), (16, bv), (18, br),
                            (20, time_decay), (22, time_first)):
                n = src.shape[0]
                ac.dma_start(rows[r0:r0 + n, :], src).then_inc(rows_in, 16)
            for w, src in enumerate((Wk, Wv, Wr, Wo)):
                ac.dma_start(w_nat[:, w, :, :], src.rearrange("(a p) h -> p a h", p=P)).then_inc(sq_in, 16)
            ac.dma_start(gw[:, :], gate_w).then_inc(gw_in, 16)
            for kc in range(KH):
                ac.dma_start(w_up[:, kc, 1, P:].rearrange("p (e m) -> p e m", m=M),
                             Wu[:, kc * P:(kc + 1) * P, :].rearrange("e p m -> p e m")).then_inc(up_in, 16)
                ac.dma_start(w_up[:, kc, 1, 0:P], sWu[kc * P:(kc + 1) * P, :]).then_inc(up_in, 16)
            nc.scalar.preload_act_table_set(SILU_SET)
            ac.wait_ge(cols_done, 1)
            nc.scalar.activation(condT[:, :], cols[:, 0:2 * B], ACT.Silu).then_inc(cond_done, 1)
            nc.scalar.preload_act_table_set(EXP_SET)
            nc.scalar.activation(decay[:, :], col["td"], ACT.Exp).then_inc(decay_done, 1)
            normalise(norm1, x_in[0], chunk(0), pick_mod=False)
            ac.wait_ge(modc_done, 4)
            pick(norm1, chunk(0))
            for kc in range(KH):
                affine1(chunk(0), kc)
            ac.wait_ge(rest_done, 1)
            for w in range(3):
                part_mix(chunk(0), w)
            for w in range(4):
                ac.wait_ge(w_turned, w + 1)
                nc.scalar.activation(WT[:, w, :, :], mm[w][:, :].rearrange("p (k h) -> p k h", k=KH),
                                     ACT.Identity, scale=-0.5 if w == O else 1.0).then_inc(wt_done, 1)
            ac.wait_ge(w_turned, 5)
            for dst in (gw_hl[:, :, 0:E], gwT[:, :, :]):
                nc.scalar.activation(dst, cb[:, 0:KH * E].rearrange("p (k e) -> p k e", k=KH),
                                     ACT.Identity).then_inc(gwt_done, 1)
            project_and_scan(chunk(0))
            ac.wait_ge(up_in, 8 * 16)
            for kc in range(KH):
                for gu in range(2):
                    nc.scalar.activation(w_up_h[:, kc, gu, :], w_up[:, kc, gu, :], ACT.Identity
                                         ).then_inc(up_hi_done, 1)
            step(None, chunk(0), chunk(1))
            with ac.Fori(0, 3) as i:
                for offset in (1, 2):
                    step(*(chunk_in_loop(i, offset + d) for d in (-1, 0, 1)))
            step(chunk(NC - 2), chunk(NC - 1), None)
            nc.scalar.preload_act_table_set(SILU_SET)
            for e in range(NB):
                silu(chunk(NC - 1), e)
                if e == 0:
                    comb_out(chunk(NC - 1))

        @block.tensor
        def _(pe):
            def turn(norm, c, kc, dst):
                for t in range(TT):
                    last = nc.tensor.transpose(dst[:, t * P:(t + 1) * P], norm.xn[:, t, kc * P:(kc + 1) * P],
                                               ident[:, :])
                last.then_inc(norm.turned, 1)

            def turn1(c, kc, first=False):
                if kc == 0:
                    pe.wait_ge(norm1.xn_done, TT * (c.n + 1))
                    if not first:
                        pe.wait_ge(route_step, ROUTE_STEPS * (c.n - 2) + 1)
                else:
                    pe.wait_ge(norm1.h_done, KH * c.n + 1)
                turn(norm1, c, kc, tp)

            def turn2(c):
                pe.wait_ge(norm2.xn_done, TT * (c.n + 1))
                turn(norm2, c, 0, tp)
                turn(norm2, c, 1, cb)

            def project(c, parts, first=False):
                for j in parts:
                    w, oc = divmod(j, KH)
                    if oc == 0:
                        pe.wait_ge(mixed_done, 3 * KH * c.n + KH * (w + 1))
                    if j >= 4:
                        pe.wait_ge(kvr_done, 3 * KH * c.n + j - 3)
                    elif not first:
                        if j % 2 == 0:
                            pe.wait_ge(silu_done, NB * (c.n - 2) + 4 + j // 2)
                        else:
                            pe.wait_ge(prod_done, NB * (c.n - 2) + 4 + j // 2)
                    for kc in range(KH):
                        last = nc.tensor.matmul(mm[j % 4][:, :], WT[:, w, kc, oc * P:(oc + 1) * P],
                                                mixed[:, w, kc, :], start=(kc == 0), stop=(kc == KH - 1))
                    last.then_inc(kvr_mm, 1)

            def output(c, tiles):
                pe.wait_ge(rw_done, c.n + 1)
                for t in tiles:
                    dst = yo[t // 2][:, (t % 2) * H:(t % 2 + 1) * H]
                    nc.tensor.matmul(dst, ones_r[:, :], bias_r[:, c.batch, :], start=True, stop=False)
                    for kc in range(KH):
                        last = nc.tensor.matmul(dst, rw[:, kc, t * P:(t + 1) * P], WoG[:, c.batch, kc, :],
                                                start=False, stop=(kc == KH - 1))
                last.then_inc(wo_mm, 1)

            def logits(c):
                pe.wait_ge(h2lo_done, c.n + 1)
                for t in range(TT):
                    at, tok = 2 * E * t, slice(t * P, (t + 1) * P)
                    for kc in range(KH):
                        nc.tensor.matmul(tp[:, at:at + 2 * E], h2_h[:, kc, tok], gw_hl[:, kc, :],
                                         start=(kc == 0), stop=False, skip_group_check=True)
                        last = nc.tensor.matmul(tp[:, at:at + E], h2_l[:, kc, tok], gw_hl[:, kc, 0:E],
                                                start=False, stop=(kc == KH - 1), skip_group_check=True)
                last.then_inc(logits_mm, 1)

            def turn_comb(c):
                pe.wait_ge(comb_done, c.n + 1)
                for t in range(TT):
                    last = nc.tensor.transpose(cb[0:2 * E, t * P:(t + 1) * P], comb[:, t, :].bitcast(F32),
                                               ident[:, :])
                last.then_inc(comb_turned, 1)

            def up(c, i, after_up=False):
                e, gu = divmod(i, 2)
                if i == 0:
                    pe.wait_ge(h2lo_done, c.n + 1)
                if i >= 4 or after_up:
                    pe.wait_ge(prod_done if gu else silu_done, NB * c.n + (e - 1 if i >= 4 else 0))
                else:
                    pe.wait_ge(kvr_done, 3 * KH * (c.n + 1) + 3 + i)
                n = 0
                for w, rhs in ((w_up_h, h2_h), (w_up_h, h2_l), (w_up_l, h2_h)):
                    for kc in range(KH):
                        last = nc.tensor.matmul(mm[(6 + i) % 4][:, :], w[:, kc, gu, e * P:(e + 1) * P],
                                                rhs[:, kc, :], start=(n == 0), stop=(n == 3 * KH - 1))
                        n += 1
                last.then_inc(up_mm, 1)

            def spread_comb(c, e):
                if e == 1:
                    pe.wait_ge(combT_done, c.n + 1)
                else:
                    pe.wait_ge(act_done, NP * c.n + min(e - 1, 2))
                nc.tensor.matmul(comb_bank[e][:, :], sel[:, e - 1, :], combT[:, :], start=True, stop=True
                                 ).then_inc(comb_mm, 1)

            def down(c, t, last_chunk=False):
                if t == 0:
                    pe.wait_ge(act_done, NP * (c.n + 1))
                    pe.wait_ge(prod_done, NB * (c.n + 1))
                    if last_chunk:
                        pe.wait_ge(x2_done, 2 * c.n)
                    else:
                        pe.wait_ge(x1_done, 2 * (c.n + 2))
                for e in range(NB):
                    last = nc.tensor.matmul(yo[t // 2][:, (t % 2) * H:(t % 2 + 1) * H],
                                            act[:, e, t * P:(t + 1) * P], WdG[:, c.batch, e, :],
                                            start=(e == 0), stop=(e == NB - 1))
                if t % 2:
                    last.then_inc(down_mm, 1)

            def step(prev, cur, nxt):
                if prev:
                    for i in range(4):
                        up(prev, i)
                    turn_comb(prev)
                    up(prev, 4)
                    spread_comb(prev, 1)
                    up(prev, 5)
                if prev:
                    up(prev, 6)
                    spread_comb(prev, 2)
                    up(prev, 7)
                if nxt:
                    turn1(nxt, 0)
                output(cur, (0, 1))
                if prev:
                    spread_comb(prev, 3)
                if nxt:
                    turn1(nxt, 1)
                output(cur, (2, 3))
                if prev:
                    up(prev, 8)
                    up(prev, 9)
                    if nxt:
                        pe.wait_ge(norm1.h_done, KH * (nxt.n + 1))
                    spread_comb(prev, 4)
                if nxt:
                    project(nxt, range(2))
                if prev:
                    pe.wait_ge(act_done, NP * cur.n)
                turn2(cur)
                if nxt:
                    project(nxt, range(2, 6))
                down(prev, 0)
                logits(cur)
                for t in range(1, TT):
                    down(prev, t)

            pe.wait_ge(ident_done, 1)
            pe.wait_ge(rows_in, 9 * 16)
            nc.tensor.transpose(mm[0][:, 0:24], rows[:, :], ident[0:24, 0:24]).then_inc(cols_turned, 1)
            pe.wait_ge(cond_done, 1)
            pe.wait_ge(cond_in, 2 * 16)
            for n, q in enumerate((0, 1, 3, 4)):
                for oc in range(KH):
                    for kc in range(KH):
                        at = (n * KH + oc) * B
                        last = nc.tensor.matmul(
                            mm[1][:, at:at + B], wmod_sb[:, kc, q * H + oc * P:q * H + (oc + 1) * P],
                            condT[:, :].rearrange("p (b k) -> p k b", k=KH)[:, kc, :],
                            start=(kc == 0), stop=(kc == KH - 1))
            last.then_inc(modc_mm, 1)
            pe.wait_ge(norm1.xn_done, TT)
            turn(norm1, chunk(0), 0, tp)
            pe.wait_ge(norm1.h_done, 1)
            turn(norm1, chunk(0), 1, tp)
            pe.wait_ge(sq_in, 4 * 16)
            pe.wait_ge(modc_done, 4)
            for w in range(4):
                for kc in range(KH):
                    for oc in range(KH):
                        last = nc.tensor.transpose(mm[w][:, kc * H + oc * P:kc * H + (oc + 1) * P],
                                                   w_nat[:, w, oc, kc * P:(kc + 1) * P], ident[:, :])
                last.then_inc(w_turned, 1)
            pe.wait_ge(gw_in, 16)
            for kc in range(KH):
                last = nc.tensor.transpose(cb[:, kc * E:(kc + 1) * E], gw[:, kc * P:(kc + 1) * P],
                                           ident[0:E, 0:E])
            last.then_inc(w_turned, 1)
            pe.wait_ge(wt_done, 4)
            pe.wait_ge(init_done, 1)
            project(chunk(0), range(6), first=True)
            for b in range(B):
                if b >= 2:
                    pe.wait_ge(gates_step, 8 * (b - 1))
                for g, q in enumerate((2, 5)):
                    for kc in range(KH):
                        last = nc.tensor.matmul(
                            yo[b % 2][:, g * H:(g + 1) * H],
                            condT[:, 2 * b + kc:2 * b + kc + 1].to_broadcast([P, P]),
                            wmod_sb[:, kc, q * H:(q + 1) * H], start=(kc == 0), stop=(kc == KH - 1))
                last.then_inc(gates_mm, 1)
            turn1(chunk(1), 0, first=True)
            turn1(chunk(1), 1)
            pe.wait_ge(bias_done, 2)
            pe.wait_ge(wog_done, B)
            output(chunk(0), (0, 1))
            output(chunk(0), (2, 3))
            pe.wait_ge(kvr_done, 3 * KH)
            project(chunk(1), range(4), first=True)
            turn2(chunk(0))
            project(chunk(1), range(4, 6))
            pe.wait_ge(gwt_done, 3)
            logits(chunk(0))
            pe.wait_ge(up_lo_done, 4)
            pe.wait_ge(wdg_done, B * NB)
            with pe.Fori(0, 3) as i:
                for offset in (1, 2):
                    step(*(chunk_in_loop(i, offset + d) for d in (-1, 0, 1)))
            step(chunk(NC - 2), chunk(NC - 1), None)
            last = chunk(NC - 1)
            for i in range(2 * NB):
                up(last, i, after_up=True)
                if i == 1:
                    turn_comb(last)
                if i > 2 and i % 2:
                    spread_comb(last, i // 2)
            for t in range(TT):
                down(last, t, last_chunk=True)

        @block.vector
        def _(ve):
            def stats(norm, src, c, ready):
                wait(ve, norm.rstd_done, c.n)
                wait(ve, ready[0], ready[1])
                for t in range(TT):
                    nc.vector.bn_stats(norm.stats[:, t, :], src[:, t, :]).then_inc(norm.bn_done, 1)
                ve.wait_ge(norm.bn_done, TT * (c.n + 1))
                nc.vector.memset(pace[:, :], 0.0)
                for t in range(TT):
                    nc.vector.bn_aggr(norm.mv[:, t, :], norm.stats[:, t, :]).then_inc(norm.mv_done, 1)

            def stats1(c):
                stats(norm1, x_in[c.half], c, (x_loaded[c.half], 16 * (c.batch + 1)))

            def mix(c, w):
                for kc in range(KH):
                    ve.wait_ge(part_mixed, 3 * KH * c.n + KH * w + kc + 1)
                    nc.vector.scalar_tensor_tensor(
                        out=mixed[:, w, kc, :], in0=hT[c.half][:, kc, 1:CH + 1],
                        scalar=mix_cols[w][:, kc:kc + 1], in1=mixed[:, w, kc, :],
                        op0=ALU.mult, op1=ALU.add).then_inc(mixed_done, 1)

            def scan_max(c):
                if c.half:
                    nc.vector.tensor_copy(state[:, :, :, 0:1], state[:, :, :, CH:CH + 1]).then_inc(seed_done, 1)
                else:
                    nc.vector.memset(state[:, 0, :, 0:1], START)
                    nc.vector.memset(state[:, 1:3, :, 0:1], 0.0).then_inc(seed_done, 1)
                ve.wait_ge(seed_done, c.n + 1)
                for h in range(KH):
                    ve.wait_ge(kvr_done, 3 * KH * c.n + h + 1)
                    nc.vector.tensor_tensor_scan(state[:, 0, h, 1:CH + 1],
                                                 decay[:, h:h + 1].to_broadcast([P, CH]),
                                                 kvr[:, K, h, :], state[:, 0, h, 0:1], ALU.add, ALU.max
                                                 ).then_inc(pp_done, 1)

                def state_arg(h):
                    ve.wait_ge(pp_done, KH * c.n + h + 1)
                    nc.vector.scalar_tensor_tensor(out=arg[:, 0, h, :], in0=state[:, 0, h, 0:CH],
                                                   scalar=decay[:, h:h + 1], in1=state[:, 0, h, 1:CH + 1],
                                                   op0=ALU.add, op1=ALU.subtract).then_inc(arg_done, 1)

                state_arg(0)
                ve.wait_ge(pp_done, KH * (c.n + 1))
                nc.vector.tensor_tensor(arg[:, 1, :, :], kvr[:, K, :, :], state[:, 0, :, 1:CH + 1],
                                        ALU.subtract).then_inc(arg_done, 1)
                state_arg(1)
                for h in range(KH):
                    nc.vector.scalar_tensor_tensor(out=tmp[:, h, :], in0=kvr[:, K, h, :],
                                                   scalar=col["tf"][:, h:h + 1], in1=state[:, 0, h, 0:CH],
                                                   op0=ALU.add, op1=ALU.subtract).then_inc(arg_done, 1)

            e1_state, e2_state, e1_out, e2_out = (arg[:, j, :, :] for j in range(4))
            v_all, aa_prev, bb_prev = kvr[:, V, :, :], state[:, 1, :, 0:CH], state[:, 2, :, 0:CH]

            def scan_bb(c):
                ve.wait_ge(kvr_done, 3 * KH * c.n + 2 * KH)
                ve.wait_ge(exp_done, 4 * c.n + 1)
                nc.vector.tensor_tensor(ev[:, :, :], e2_state, v_all, ALU.mult).then_inc(ev_done, 1)
                ve.wait_ge(exp_done, 4 * c.n + 2)
                for h in range(KH):
                    nc.vector.tensor_tensor_scan(state[:, 2, h, 1:CH + 1], arg[:, 0, h, :], arg[:, 1, h, :],
                                                 state[:, 2, h, 0:1], ALU.mult, ALU.add).then_inc(bb_done, 1)

            def scan_aa(c):
                ve.wait_ge(ev_done, c.n + 1)
                for h in range(KH):
                    nc.vector.tensor_tensor_scan(state[:, 1, h, 1:CH + 1], arg[:, 0, h, :], ev[:, h, :],
                                                 state[:, 1, h, 0:1], ALU.mult, ALU.add).then_inc(aa_done, 1)

            def out_sums(c, n):
                if n == 0:
                    ve.wait_ge(exp_done, 4 * c.n + 3)
                    ve.wait_ge(bb_done, KH * (c.n + 1))
                    nc.vector.tensor_tensor(den, e1_out, bb_prev, ALU.mult).then_inc(part_done, 1)
                elif n == 1:
                    ve.wait_ge(aa_done, KH * (c.n + 1))
                    nc.vector.tensor_tensor(num, e1_out, aa_prev, ALU.mult).then_inc(part_done, 1)
                elif n == 2:
                    ve.wait_ge(exp_done, 4 * c.n + 4)
                    ve.wait_ge(part_done, 3 * c.n + 1)
                    nc.vector.tensor_tensor(den, den, e2_out, ALU.add).then_inc(den_done, 1)
                elif n == 3:
                    nc.vector.tensor_tensor(ev[:, :, :], e2_out, v_all, ALU.mult).then_inc(part_done, 1)
                else:
                    ve.wait_ge(part_done, 3 * c.n + 3)
                    nc.vector.tensor_tensor(num, num, ev[:, :, :], ALU.add).then_inc(num_done, 1)

            def divide(c, n):
                if n == 0:
                    ve.wait_ge(rec_done, c.n + 1)
                    nc.vector.tensor_tensor(tmp[:, :, :], den, rec, ALU.mult).then_inc(newton_done, 1)
                elif n == 1:
                    ve.wait_ge(num_done, c.n + 1)
                    nc.vector.tensor_tensor(ev[:, :, :], num, rec, ALU.mult).then_inc(newton_done, 1)
                elif n == 2:
                    ve.wait_ge(newton_done, 3 * c.n + 2)
                    nc.vector.scalar_tensor_tensor(out=num, in0=tmp[:, :, :], scalar=2.0, in1=ev[:, :, :],
                                                   op0=ALU.subtract, op1=ALU.mult).then_inc(newton_done, 1)
                else:
                    ve.wait_ge(newton_done, 3 * c.n + 3)
                    ve.wait_ge(sgm_done, c.n + 1)
                    nc.vector.scalar_tensor_tensor(out=rw, in0=sgm, scalar=1.0, in1=num,
                                                   op0=ALU.add, op1=ALU.mult).then_inc(rw_done, 1)

            def residual1(c, k):
                if k == 0:
                    ve.wait_ge(stored[c.half], 16 * (c.batch + 1))
                ve.wait_ge(wo_mm, 2 * c.n + k + 1)
                nc.vector.tensor_tensor(
                    x1[c.half][:, 2 * k:2 * k + 2, :], yo[k][:, :].rearrange("p (t h) -> p t h", t=2),
                    x_in[c.half][:, 2 * k:2 * k + 2, :], ALU.add).then_inc(x1_done, 1)

            def residual2(c, k):
                ve.wait_ge(down_mm, 2 * c.n + k + 1)
                nc.vector.tensor_tensor(
                    x1[c.half][:, 2 * k:2 * k + 2, :], yo[k][:, :].rearrange("p (t h) -> p t h", t=2),
                    x1[c.half][:, 2 * k:2 * k + 2, :], ALU.add).then_inc(x2_done, 1)

            def low_part(c):
                ve.wait_ge(norm2.h_done, KH * (c.n + 1))
                nc.vector.tensor_tensor(h2_l[:, :, :], h2, h2_h[:, :, :].bitcast(F32), ALU.subtract
                                        ).then_inc(h2lo_done, 1)

            def route(c, n):
                lg, eq, pr, m1, l2, m2, w1m, w2m, both = (rt[:, j, :, :] for j in range(9))
                v1, v2, gap, ex, p1, s, w1, w2 = (r1[:, j, :] for j in range(8))
                wide = lambda v: v.unsqueeze(2).to_broadcast([P, TT, E])
                V = nc.vector
                if n:
                    ve.wait_ge(route_step, ROUTE_STEPS * c.n + n)
                if n == 0:
                    ve.wait_ge(logits_mm, c.n + 1)
                    ins = V.tensor_reduce(lg, tp[:, 0:2 * TT * E].rearrange("p (t a e) -> p t e a", a=2, e=E),
                                          AX.X, ALU.add)
                elif n == 1:
                    ins = V.tensor_reduce(v1, lg, AX.X, ALU.max)
                elif n == 2:
                    ins = V.tensor_tensor(eq, lg, wide(v1), ALU.is_equal)
                elif n == 3:
                    ins = V.tensor_tensor(pr, eq, prio[:, :, :], ALU.mult)
                elif n == 4:
                    ins = V.tensor_reduce(s, pr, AX.X, ALU.max)
                elif n == 5:
                    ins = V.tensor_tensor(m1, prio[:, :, :], wide(s), ALU.is_equal)
                elif n == 6:
                    ins = V.scalar_tensor_tensor(out=l2, in0=m1, scalar=-3e38, in1=lg,
                                                 op0=ALU.mult, op1=ALU.add)
                elif n == 7:
                    ins = V.tensor_reduce(v2, l2, AX.X, ALU.max)
                elif n == 8:
                    V.tensor_tensor(gap, v2, v1, ALU.subtract).then_inc(gap_done, 1)
                    ins = V.tensor_tensor(eq, l2, wide(v2), ALU.is_equal)
                elif n == 9:
                    ins = V.tensor_tensor(pr, eq, prio[:, :, :], ALU.mult)
                elif n == 10:
                    ins = V.tensor_reduce(s, pr, AX.X, ALU.max)
                elif n == 11:
                    ins = V.tensor_tensor(m2, prio[:, :, :], wide(s), ALU.is_equal)
                elif n == 12:
                    ve.wait_ge(gap_exp, c.n + 1)
                    ins = V.tensor_scalar(p1, ex, 1.0, None, ALU.add)
                elif n == 13:
                    ins = V.reciprocal(w1, p1)
                elif n == 14:
                    ins = V.tensor_tensor(w2, ex, w1, ALU.mult)
                elif n == 15:
                    ins = V.tensor_tensor(w1m, m1, wide(w1), ALU.mult)
                elif n == 16:
                    ins = V.tensor_tensor(w2m, m2, wide(w2), ALU.mult)
                elif n == 17:
                    ins = V.tensor_tensor(both, w1m, w2m, ALU.add)
                elif n == 18:
                    ins = V.tensor_copy(comb[:, :, 0:E], both)
                else:
                    V.tensor_tensor(comb[:, :, E:2 * E], both, comb[:, :, 0:E].bitcast(F32), ALU.subtract
                                    ).then_inc(comb_done, 1)
                    return
                ins.then_inc(route_step, 1)

            def route_all(c):
                for n in range(ROUTE_STEPS + 1):
                    route(c, n)

            def gate_up(c, e):
                ve.wait_ge(silu_done, NB * c.n + e + 1)
                ve.wait_ge(up_mm, 2 * (NB * c.n + e) + 2)
                dst = sg if e else act
                nc.vector.tensor_tensor(dst[:, e, :], mm[(7 + 2 * e) % 4][:, :], sg[:, e, :], ALU.mult
                                        ).then_inc(prod_done, 1)

            def weigh(c, e):
                ve.wait_ge(comb_mm, NP * c.n + e)
                ve.wait_ge(prod_done, NB * c.n + e + 1)
                nc.vector.tensor_tensor(act[:, e, :], comb_bank[e][:, :], sg[:, e, :], ALU.mult).then_inc(act_done, 1)

            def step(prev, cur, nxt):
                if prev:
                    gate_up(prev, 0)
                if nxt:
                    stats1(nxt)
                divide(cur, 0)
                divide(cur, 1)
                if prev:
                    gate_up(prev, 1)
                divide(cur, 2)
                if prev:
                    weigh(prev, 1)
                divide(cur, 3)
                if prev:
                    gate_up(prev, 2)
                    weigh(prev, 2)
                if prev:
                    gate_up(prev, 3)
                residual1(cur, 0)
                if prev:
                    weigh(prev, 3)
                residual1(cur, 1)
                stats(norm2, x1[cur.half], cur, (x1_done, 2 * (cur.n + 1)))
                if nxt:
                    mix(nxt, 0)
                    mix(nxt, 1)
                if prev:
                    gate_up(prev, 4)
                    weigh(prev, 4)
                if nxt:
                    mix(nxt, 2)
                    scan_max(nxt)
                    scan_bb(nxt)
                low_part(cur)
                if nxt:
                    scan_aa(nxt)
                    for n in range(5):
                        out_sums(nxt, n)
                        for k in range(3 * n, 3 * n + 3):
                            route(cur, k)
                    residual2(prev, 0)
                    for k in range(15, ROUTE_STEPS + 1):
                        route(cur, k)
                else:
                    residual2(prev, 0)
                    route_all(cur)
                residual2(prev, 1)

            for e in range(E):
                nc.vector.memset(prio[:, :, e], float(E - e))
            nc.vector.memset(hT[0][:, :, 0:1], 0.0)
            nc.vector.memset(gmag[:, 0, 0, 0:P], 1.0).then_inc(bias_step, 1)
            nc.vector.memset(bias_r[:, :, :].bitcast(F32), 0.0).then_inc(bias_step, 1)
            ve.wait_ge(bias_step, 2)
            nc.vector.tensor_copy(ones_r[:, :], gmag[:, 0, 0, 0:P]).then_inc(bias_step, 1)
            ve.wait_ge(sel_done, 2)
            nc.vector.tensor_copy(sel[:, :, :], sel_f[:, :, :]).then_inc(init_done, 1)
            ve.wait_ge(cols_turned, 1)
            nc.vector.tensor_copy(cols[:, :], mm[0][:, 0:24]).then_inc(cols_done, 1)
            ve.wait_ge(cols_done, 1)
            nc.vector.tensor_scalar(rest[:, :], cols[:, 2 * B:2 * B + 3 * KH], -1.0, 1.0, ALU.mult, ALU.add
                                    ).then_inc(rest_done, 1)
            stats1(chunk(0))
            ve.wait_ge(modc_mm, 1)
            for n in range(4):
                nc.vector.tensor_scalar(modc[:, n, :, :],
                                        mm[1][:, n * KH * B:(n + 1) * KH * B].rearrange("p (k b) -> p k b", b=B),
                                        float(n % 2), None, ALU.add).then_inc(modc_done, 1)
            ve.wait_ge(decay_done, 1)
            nc.vector.tensor_scalar(decay[:, :], decay[:, :], -1.0, None, ALU.mult).then_inc(decay_done, 1)
            for w in range(3):
                mix(chunk(0), w)
            ve.wait_ge(decay_done, 2)
            scan_max(chunk(0))
            scan_bb(chunk(0))
            scan_aa(chunk(0))
            for n in range(5):
                out_sums(chunk(0), n)
            stats1(chunk(1))
            ve.wait_ge(bias_step, 3)
            for b in range(B):
                ve.wait_ge(gates_mm, b + 1)
                raw = yo[b % 2][:, :].rearrange("p (g h) -> p g h", g=2)
                for g, dst in enumerate((ga, gb)):
                    nc.vector.tensor_scalar(dst[:, b, :], raw[:, g, :], 0.0, 2.0, ALU.is_ge, ALU.mult
                                            ).then_inc(gates_step, 1)
                for g, dst in enumerate((ga, gb)):
                    ve.wait_ge(gates_step, 8 * b + g + 1)
                    nc.vector.scalar_tensor_tensor(out=gmag[:, b % 2, g, :], in0=dst[:, b, :], scalar=1.0,
                                                   in1=raw[:, g, :], op0=ALU.subtract, op1=ALU.mult
                                                   ).then_inc(gates_step, 1)
                for g in range(2):
                    ve.wait_ge(gates_step, 8 * b + g + 3)
                    nc.vector.tensor_scalar(gmag[:, b % 2, g, :], gmag[:, b % 2, g, :], 0.25, None, ALU.max
                                            ).then_inc(gates_step, 1)
                for g, dst in enumerate((ga, gb)):
                    ve.wait_ge(gates_step, 8 * b + g + 5)
                    nc.vector.scalar_tensor_tensor(out=dst[:, b, :], in0=dst[:, b, :], scalar=1.0,
                                                   in1=gmag[:, b % 2, g, :], op0=ALU.subtract, op1=ALU.mult
                                                   ).then_inc(gates_step, 1)
            ve.wait_ge(gates_step, 8 * B)
            ve.wait_ge(bo_in, 16)
            ve.wait_ge(wt_done, 4)
            for b in range(B):
                nc.vector.tensor_tensor(WoG[:, b, :, :], WT[:, O, :, :],
                                        ga[:, b, :].unsqueeze(1).to_broadcast([P, KH, H]), ALU.mult
                                        ).then_inc(wog_done, 1)
            ve.wait_ge(wog_done, B)
            nc.vector.tensor_tensor(gabo[:, :, :], ga[:, :, :], bo_b[:, :].unsqueeze(1).to_broadcast([P, B, H]),
                                    ALU.mult).then_inc(gates_done, 1)
            ve.wait_ge(gates_done, 1)
            nc.vector.tensor_copy(bias_r[0:1, :, :], gabo[0:1, :, :]).then_inc(bias_done, 1)
            nc.vector.tensor_copy(bias_r[32:33, :, :], gabo[32:33, :, :]).then_inc(bias_step, 1)
            ve.wait_ge(bias_step, 4)
            nc.vector.tensor_tensor(bias_r[32:33, :, :], gabo[32:33, :, :], bias_r[32:33, :, :].bitcast(F32),
                                    ALU.subtract).then_inc(bias_done, 1)
            for n in range(4):
                divide(chunk(0), n)
            mix(chunk(1), 0)
            mix(chunk(1), 1)
            ve.wait_ge(gwt_done, 2)
            nc.vector.tensor_tensor(gw_hl[:, :, E:2 * E], gwT[:, :, :], gw_hl[:, :, 0:E].bitcast(F32),
                                    ALU.subtract).then_inc(gwt_done, 1)
            residual1(chunk(0), 0)
            residual1(chunk(0), 1)
            stats(norm2, x1[0], chunk(0), (x1_done, 2))
            mix(chunk(1), 2)
            scan_max(chunk(1))
            scan_bb(chunk(1))
            low_part(chunk(0))
            scan_aa(chunk(1))
            for n in range(5):
                for k in range(3 * n, 3 * n + 3):
                    route(chunk(0), k)
                out_sums(chunk(1), n)
            for k in range(15, ROUTE_STEPS + 1):
                route(chunk(0), k)
            with ve.Fori(0, 3) as i:
                for offset in (1, 2):
                    step(*(chunk_in_loop(i, offset + d) for d in (-1, 0, 1)))
            last = chunk(NC - 1)
            step(chunk(NC - 2), last, None)
            for e in range(NB):
                gate_up(last, e)
                if e:
                    weigh(last, e)
            for k in range(2):
                residual2(last, k)


_INS = ['L0_attn_x', 'L0_attn_Wk', 'L0_attn_bk', 'L0_attn_Wv', 'L0_attn_bv', 'L0_attn_Wr', 'L0_attn_br',
        'L0_attn_Wo', 'L0_attn_bo', 'L0_attn_tmk', 'L0_attn_tmv', 'L0_attn_tmr', 'L0_attn_time_decay',
        'L0_attn_time_first', 'L0_ffn_gate_w', 'L0_ffn_Wg', 'L0_ffn_Wu', 'L0_ffn_Wd', 'L0_ffn_sWg',
        'L0_ffn_sWu', 'L0_ffn_sWd', 'L0_c', 'L0_wmod']
_ROWS = {'L0_attn_bk', 'L0_attn_bv', 'L0_attn_br', 'L0_attn_tmk', 'L0_attn_tmv', 'L0_attn_tmr',
         'L0_attn_time_decay', 'L0_attn_time_first', 'L0_c'}


def kernel(**inputs):
    import numpy as _np
    import concourse.bacc as _bacc
    from concourse import mybir as _mybir
    from concourse.bass_utils import run_bass_kernel_spmd as _run

    nc = _bacc.Bacc("TRN2", target_bir_lowering=False, num_devices=1)
    arrays, args = {}, []
    for name in _INS:
        a = _np.ascontiguousarray(inputs[name])
        if name in _ROWS:
            a = a.reshape(-1, P)
        arrays[f"in_{name}_dram"] = a
        args.append(nc.dram_tensor(f"in_{name}_dram", a.shape, _mybir.dt.from_np(a.dtype), kind="ExternalInput").ap())
    out = nc.dram_tensor("out_0_dram", (B, T, H), F32, kind="ExternalOutput").ap()
    adaln_rwkv_moe(nc, *args, out)
    r = _run(nc, [arrays], core_ids=[0])
    return r.results[0]["out_0_dram"]
```
